# Optimizing a Trainium2 kernel written in Bass

```python
import numpy as np
import jax
import jax.numpy as jnp

def _softmax(x, axis=-1):
    return jax.nn.softmax(x, axis=axis)

def _gelu(x):
    return jax.nn.gelu(x, approximate=True)

def _silu(x):
    return jax.nn.silu(x)

def _sigmoid(x):
    return jax.nn.sigmoid(x)

def _layernorm(x, axis=-1, eps=1e-05):
    m = jnp.mean(x, axis=axis, keepdims=True)
    v = jnp.var(x, axis=axis, keepdims=True)
    return (x - m) / jnp.sqrt(v + eps)

def _scatter_add(tgt, idx, src, axis=0):
    return tgt.at[idx].add(src)

def _segment_sum(src, seg, n):
    return jax.ops.segment_sum(src, seg, n)
kernel_name = 'mk_decoder_preln_d1_seqx_r8_0c2698'

def setup_inputs(seed: int=0):
    np.random.seed(seed)
    _w = jnp.asarray

    def _rec_inputs():
        import jax
        import jax.numpy as jnp
        _rk = jax.random.key(seed)
        x = 7.22e-05 + 1 * jax.random.normal(jax.random.fold_in(_rk, 1), (4, 512, 128), jnp.float32)
        _lenS = 512 - jax.random.randint(jax.random.fold_in(_rk, 7), (4,), 0, max(1, 512 // 4) + 1, jnp.int32)
        _lenS2 = 154 - jax.random.randint(jax.random.fold_in(_rk, 8), (4,), 0, max(1, 154 // 4) + 1, jnp.int32)
        _ctx_1024P = jax.random.normal(jax.random.fold_in(_rk, 11), (4, 16, 128), jnp.float32)
        _ctx_1024c = jax.random.dirichlet(jax.random.fold_in(_rk, 511), 0.3 * jnp.ones((16,), jnp.float32), (4, 154))
        _ctx_1024t = jnp.einsum('bsk,bkd->bsd', _ctx_1024c, _ctx_1024P)
        _ctx_1024t = _ctx_1024t * jax.lax.rsqrt(jnp.mean(jnp.square(_ctx_1024t)) + 1e-12) * 0.953939
        ctx_1024 = 4.13588e-05 + 0.999923 * (_ctx_1024t + 0.3 * jax.random.normal(jax.random.fold_in(_rk, 611), (4, 154, 128), jnp.float32))
        return (x, ctx_1024)
    x, ctx_1024 = _rec_inputs()

    def _L0_attn_setup():
        import jax, jax.numpy as jnp
        import numpy as np
        from jax import lax
        B, L, DM = (4, 512, 128)
        D_INNER, D_STATE, D_CONV, DT_RANK = (256, 16, 4, 64)

        def _silu(v):
            return v * jax.nn.sigmoid(v)

        def _causal_depthwise_conv(xc, conv_w, conv_b):
            k = conv_w[:, None, :]
            y = lax.conv_general_dilated(xc, k, window_strides=(1,), padding=[(D_CONV - 1, 0)], dimension_numbers=('NCH', 'OIH', 'NCH'), feature_group_count=D_INNER)
            return y + conv_b[None, :, None]

        def _mamba_forward(x, W_in, conv_w, conv_b, W_xproj, W_dt, b_dt, A_log, Dp, W_out):
            xz = jnp.einsum('bld,de->ble', x, W_in)
            xin, z = jnp.split(xz, 2, axis=-1)
            xc = _causal_depthwise_conv(xin.transpose(0, 2, 1), conv_w, conv_b)
            xc = _silu(xc).transpose(0, 2, 1)
            x_dbl = jnp.einsum('bld,de->ble', xc, W_xproj)
            dt, Bm, Cm = jnp.split(x_dbl, [DT_RANK, DT_RANK + D_STATE], axis=-1)
            dt = jax.nn.softplus(jnp.einsum('blr,rd->bld', dt, W_dt) + b_dt)
            A = -jnp.exp(A_log)

            def step(h, inp):
                dt_t, B_t, C_t, x_t = inp
                dA = jnp.exp(dt_t[..., None] * A)
                dBx = dt_t[..., None] * B_t[:, None, :] * x_t[..., None]
                h = dA * h + dBx
                y_t = jnp.sum(h * C_t[:, None, :], axis=-1)
                return (h, y_t)
            h0 = jnp.zeros((x.shape[0], D_INNER, D_STATE), x.dtype)
            xs = (dt.transpose(1, 0, 2), Bm.transpose(1, 0, 2), Cm.transpose(1, 0, 2), xc.transpose(1, 0, 2))
            _, ys = lax.scan(step, h0, xs)
            y = ys.transpose(1, 0, 2) + xc * Dp
            y = y * _silu(z)
            return jnp.einsum('bld,de->ble', y, W_out)
        key = jax.random.key(seed)
        ks = jax.random.split(key, 8)
        s = 0.02
        x = jax.random.normal(ks[0], (B, L, DM), jnp.float32)
        W_in = jax.random.normal(ks[1], (DM, 2 * D_INNER), jnp.float32) * s
        conv_w = jax.random.normal(ks[2], (D_INNER, D_CONV), jnp.float32) * s
        conv_b = jnp.zeros((D_INNER,), jnp.float32)
        W_xproj = jax.random.normal(ks[3], (D_INNER, DT_RANK + 2 * D_STATE), jnp.float32) * s
        W_dt = jax.random.normal(ks[4], (DT_RANK, D_INNER), jnp.float32) * s
        b_dt = jnp.full((D_INNER,), -4.6, jnp.float32)
        A_log = jnp.log(jnp.broadcast_to(jnp.arange(1, D_STATE + 1, dtype=jnp.float32), (D_INNER, D_STATE)))
        Dp = jnp.ones((D_INNER,), jnp.float32)
        W_out = jax.random.normal(ks[5], (D_INNER, DM), jnp.float32) * s
        return {'x': x, 'W_in': W_in, 'conv_w': conv_w, 'conv_b': conv_b, 'W_xproj': W_xproj, 'W_dt': W_dt, 'b_dt': b_dt, 'A_log': A_log, 'Dp': Dp, 'W_out': W_out}
    _L0_attn_all = _L0_attn_setup()
    _L0_attn_in = {k: v for k, v in _L0_attn_all.items() if k in ('W_in', 'conv_w', 'conv_b', 'W_xproj', 'W_dt', 'b_dt', 'A_log', 'Dp', 'W_out')}
    del _L0_attn_all

    def _L0_xattn_setup():
        import jax, jax.numpy as jnp
        import numpy as np
        B, SD, SE, D, H = (4, 256, 256, 128, 16)
        HD = D // H

        def _mha(xq, xk, xv, Wq, bq, Wk, bk, Wv, bv, Wo, bo, causal):
            q = jnp.einsum('bsd,hde->bhse', xq, Wq) + bq[None, :, None, :]
            k = jnp.einsum('bsd,hde->bhse', xk, Wk) + bk[None, :, None, :]
            v = jnp.einsum('bsd,hde->bhse', xv, Wv) + bv[None, :, None, :]
            scale = 1.0 / jnp.sqrt(jnp.asarray(HD, q.dtype))
            scores = jnp.einsum('bhqe,bhke->bhqk', q, k) * scale
            if causal:
                mask = jnp.tril(jnp.ones((q.shape[2], k.shape[2]), bool))
                scores = jnp.where(mask, scores, jnp.finfo(scores.dtype).min)
            w = jax.nn.softmax(scores, axis=-1)
            out = jnp.einsum('bhqk,bhke->bhqe', w, v)
            out = out.transpose(0, 2, 1, 3).reshape(out.shape[0], out.shape[2], D)
            return out @ Wo + bo
        key = jax.random.key(seed)
        ks = jax.random.split(key, 19)
        sd = 1.0 / np.sqrt(D)
        n = lambda k, shape, s: jax.random.normal(k, shape, jnp.float32) * s
        inp = {'x': n(ks[0], (B, SD, D), 1.0), 'encoder_k': n(ks[1], (B, SE, D), 1.0), 'encoder_v': n(ks[2], (B, SE, D), 1.0), 'Wq1': n(ks[3], (H, D, HD), sd), 'bq1': jnp.zeros((H, HD), jnp.float32), 'Wk1': n(ks[4], (H, D, HD), sd), 'bk1': jnp.zeros((H, HD), jnp.float32), 'Wv1': n(ks[5], (H, D, HD), sd), 'bv1': jnp.zeros((H, HD), jnp.float32), 'Wo1': n(ks[6], (D, D), sd), 'bo1': jnp.zeros((D,), jnp.float32), 'Wq2': n(ks[7], (H, D, HD), sd), 'bq2': jnp.zeros((H, HD), jnp.float32), 'Wk2': n(ks[8], (H, D, HD), sd), 'bk2': jnp.zeros((H, HD), jnp.float32), 'Wv2': n(ks[9], (H, D, HD), sd), 'bv2': jnp.zeros((H, HD), jnp.float32), 'Wo2': n(ks[10], (D, D), sd), 'bo2': jnp.zeros((D,), jnp.float32)}
        return inp
    _L0_xattn_all = _L0_xattn_setup()
    _L0_xattn_in = {k: v for k, v in _L0_xattn_all.items() if k in ('Wq1', 'bq1', 'Wk1', 'bk1', 'Wv1', 'bv1', 'Wo1', 'bo1', 'Wq2', 'bq2', 'Wk2', 'bk2', 'Wv2', 'bv2', 'Wo2', 'bo2')}
    del _L0_xattn_all

    def _L0_ffn_setup():
        import jax, jax.numpy as jnp
        import numpy as np
        H, E, DFF = (128, 8, 512)
        key = jax.random.key(seed)
        ks = jax.random.split(key, 7)
        s = lambda *shape: 1.0 / np.sqrt(shape[-2] if len(shape) > 1 else shape[-1])
        x = jax.random.normal(ks[0], (2, 256, H), dtype=jnp.float32)
        Wr = jax.random.normal(ks[1], (H, E), dtype=jnp.float32) * (1.0 / np.sqrt(H))
        br = jnp.zeros((E,), dtype=jnp.float32)
        W1 = jax.random.normal(ks[2], (E, H, DFF), dtype=jnp.float32) * (1.0 / np.sqrt(H))
        b1 = jnp.zeros((E, DFF), dtype=jnp.float32)
        W2 = jax.random.normal(ks[3], (E, DFF, H), dtype=jnp.float32) * (1.0 / np.sqrt(DFF))
        b2 = jnp.zeros((E, H), dtype=jnp.float32)
        return {'x': x, 'Wr': Wr, 'br': br, 'W1': W1, 'b1': b1, 'W2': W2, 'b2': b2}
    _L0_ffn_all = _L0_ffn_setup()
    _L0_ffn_in = {k: v for k, v in _L0_ffn_all.items() if k in ('Wr', 'br', 'W1', 'b1', 'W2', 'b2')}
    del _L0_ffn_all
    return {'x': x, 'ctx_1024': ctx_1024, 'L0_attn_W_in': _L0_attn_in['W_in'], 'L0_attn_conv_w': _L0_attn_in['conv_w'], 'L0_attn_conv_b': _L0_attn_in['conv_b'], 'L0_attn_W_xproj': _L0_attn_in['W_xproj'], 'L0_attn_W_dt': _L0_attn_in['W_dt'], 'L0_attn_b_dt': _L0_attn_in['b_dt'], 'L0_attn_A_log': _L0_attn_in['A_log'], 'L0_attn_Dp': _L0_attn_in['Dp'], 'L0_attn_W_out': _L0_attn_in['W_out'], 'L0_xattn_Wq1': _L0_xattn_in['Wq1'], 'L0_xattn_bq1': _L0_xattn_in['bq1'], 'L0_xattn_Wk1': _L0_xattn_in['Wk1'], 'L0_xattn_bk1': _L0_xattn_in['bk1'], 'L0_xattn_Wv1': _L0_xattn_in['Wv1'], 'L0_xattn_bv1': _L0_xattn_in['bv1'], 'L0_xattn_Wo1': _L0_xattn_in['Wo1'], 'L0_xattn_bo1': _L0_xattn_in['bo1'], 'L0_xattn_Wq2': _L0_xattn_in['Wq2'], 'L0_xattn_bq2': _L0_xattn_in['bq2'], 'L0_xattn_Wk2': _L0_xattn_in['Wk2'], 'L0_xattn_bk2': _L0_xattn_in['bk2'], 'L0_xattn_Wv2': _L0_xattn_in['Wv2'], 'L0_xattn_bv2': _L0_xattn_in['bv2'], 'L0_xattn_Wo2': _L0_xattn_in['Wo2'], 'L0_xattn_bo2': _L0_xattn_in['bo2'], 'L0_ffn_Wr': _L0_ffn_in['Wr'], 'L0_ffn_br': _L0_ffn_in['br'], 'L0_ffn_W1': _L0_ffn_in['W1'], 'L0_ffn_b1': _L0_ffn_in['b1'], 'L0_ffn_W2': _L0_ffn_in['W2'], 'L0_ffn_b2': _L0_ffn_in['b2']}

def reference(x, ctx_1024, L0_attn_W_in, L0_attn_conv_w, L0_attn_conv_b, L0_attn_W_xproj, L0_attn_W_dt, L0_attn_b_dt, L0_attn_A_log, L0_attn_Dp, L0_attn_W_out, L0_xattn_Wq1, L0_xattn_bq1, L0_xattn_Wk1, L0_xattn_bk1, L0_xattn_Wv1, L0_xattn_bv1, L0_xattn_Wo1, L0_xattn_bo1, L0_xattn_Wq2, L0_xattn_bq2, L0_xattn_Wk2, L0_xattn_bk2, L0_xattn_Wv2, L0_xattn_bv2, L0_xattn_Wo2, L0_xattn_bo2, L0_ffn_Wr, L0_ffn_br, L0_ffn_W1, L0_ffn_b1, L0_ffn_W2, L0_ffn_b2):
    import jax
    import jax.numpy as jnp

    def _L0_attn_ref(x, W_in, conv_w, conv_b, W_xproj, W_dt, b_dt, A_log, Dp, W_out):
        import jax, jax.numpy as jnp
        import numpy as np
        from jax import lax
        B, L, DM = (4, 512, 128)
        D_INNER, D_STATE, D_CONV, DT_RANK = (256, 16, 4, 64)

        def _silu(v):
            return v * jax.nn.sigmoid(v)

        def _causal_depthwise_conv(xc, conv_w, conv_b):
            k = conv_w[:, None, :]
            y = lax.conv_general_dilated(xc, k, window_strides=(1,), padding=[(D_CONV - 1, 0)], dimension_numbers=('NCH', 'OIH', 'NCH'), feature_group_count=D_INNER)
            return y + conv_b[None, :, None]

        def _mamba_forward(x, W_in, conv_w, conv_b, W_xproj, W_dt, b_dt, A_log, Dp, W_out):
            xz = jnp.einsum('bld,de->ble', x, W_in)
            xin, z = jnp.split(xz, 2, axis=-1)
            xc = _causal_depthwise_conv(xin.transpose(0, 2, 1), conv_w, conv_b)
            xc = _silu(xc).transpose(0, 2, 1)
            x_dbl = jnp.einsum('bld,de->ble', xc, W_xproj)
            dt, Bm, Cm = jnp.split(x_dbl, [DT_RANK, DT_RANK + D_STATE], axis=-1)
            dt = jax.nn.softplus(jnp.einsum('blr,rd->bld', dt, W_dt) + b_dt)
            A = -jnp.exp(A_log)

            def step(h, inp):
                dt_t, B_t, C_t, x_t = inp
                dA = jnp.exp(dt_t[..., None] * A)
                dBx = dt_t[..., None] * B_t[:, None, :] * x_t[..., None]
                h = dA * h + dBx
                y_t = jnp.sum(h * C_t[:, None, :], axis=-1)
                return (h, y_t)
            h0 = jnp.zeros((x.shape[0], D_INNER, D_STATE), x.dtype)
            xs = (dt.transpose(1, 0, 2), Bm.transpose(1, 0, 2), Cm.transpose(1, 0, 2), xc.transpose(1, 0, 2))
            _, ys = lax.scan(step, h0, xs)
            y = ys.transpose(1, 0, 2) + xc * Dp
            y = y * _silu(z)
            return jnp.einsum('bld,de->ble', y, W_out)
        return _mamba_forward(x, W_in, conv_w, conv_b, W_xproj, W_dt, b_dt, A_log, Dp, W_out)

    def _L0_xattn_ref(x, encoder_k, encoder_v, Wq1, bq1, Wk1, bk1, Wv1, bv1, Wo1, bo1, Wq2, bq2, Wk2, bk2, Wv2, bv2, Wo2, bo2):
        import jax, jax.numpy as jnp
        import numpy as np
        B, SD, SE, D, H = (4, 256, 256, 128, 16)
        HD = D // H

        def _mha(xq, xk, xv, Wq, bq, Wk, bk, Wv, bv, Wo, bo, causal):
            q = jnp.einsum('bsd,hde->bhse', xq, Wq) + bq[None, :, None, :]
            k = jnp.einsum('bsd,hde->bhse', xk, Wk) + bk[None, :, None, :]
            v = jnp.einsum('bsd,hde->bhse', xv, Wv) + bv[None, :, None, :]
            scale = 1.0 / jnp.sqrt(jnp.asarray(HD, q.dtype))
            scores = jnp.einsum('bhqe,bhke->bhqk', q, k) * scale
            if causal:
                mask = jnp.tril(jnp.ones((q.shape[2], k.shape[2]), bool))
                scores = jnp.where(mask, scores, jnp.finfo(scores.dtype).min)
            w = jax.nn.softmax(scores, axis=-1)
            out = jnp.einsum('bhqk,bhke->bhqe', w, v)
            out = out.transpose(0, 2, 1, 3).reshape(out.shape[0], out.shape[2], D)
            return out @ Wo + bo
        h = _mha(x, x, x, Wq1, bq1, Wk1, bk1, Wv1, bv1, Wo1, bo1, causal=True)
        out = _mha(h, encoder_k, encoder_v, Wq2, bq2, Wk2, bk2, Wv2, bv2, Wo2, bo2, causal=False)
        return out

    def _L0_ffn_ref(x, Wr, br, W1, b1, W2, b2):
        import jax, jax.numpy as jnp
        import numpy as np
        H, E, DFF = (128, 8, 512)
        B, S, Hd = x.shape
        n_exp = W1.shape[0]
        xt = x.reshape(-1, Hd)
        logits = xt @ Wr + br
        probs = jax.nn.softmax(logits, axis=-1)
        gate = jnp.max(probs, axis=-1)
        idx = jnp.argmax(probs, axis=-1)
        h1 = jnp.maximum(jnp.einsum('th,ehf->etf', xt, W1) + b1[:, None, :], 0.0)
        ye = jnp.einsum('etf,efh->eth', h1, W2) + b2[:, None, :]
        onehot = jax.nn.one_hot(idx, n_exp, dtype=xt.dtype)
        y = jnp.einsum('te,eth->th', onehot, ye) * gate[:, None]
        return y.reshape(B, S, Hd)
    x = x + _L0_attn_ref(_layernorm(x, axis=-1), L0_attn_W_in, L0_attn_conv_w, L0_attn_conv_b, L0_attn_W_xproj, L0_attn_W_dt, L0_attn_b_dt, L0_attn_A_log, L0_attn_Dp, L0_attn_W_out)
    x = x + _L0_xattn_ref(_layernorm(x, axis=-1), ctx_1024, ctx_1024, L0_xattn_Wq1, L0_xattn_bq1, L0_xattn_Wk1, L0_xattn_bk1, L0_xattn_Wv1, L0_xattn_bv1, L0_xattn_Wo1, L0_xattn_bo1, L0_xattn_Wq2, L0_xattn_bq2, L0_xattn_Wk2, L0_xattn_bk2, L0_xattn_Wv2, L0_xattn_bv2, L0_xattn_Wo2, L0_xattn_bo2)
    x = x + _L0_ffn_ref(_layernorm(x, axis=-1), L0_ffn_Wr, L0_ffn_br, L0_ffn_W1, L0_ffn_b1, L0_ffn_W2, L0_ffn_b2)
    return x

_drawn_inputs = setup_inputs


def setup_inputs(seed=0):
    import zlib

    import numpy as np

    out = dict(_drawn_inputs(seed))
    spreads = {'L0_attn_conv_b': (0.0, 0.8),
     'L0_attn_b_dt': (-4.599999904632568, 0.6),
     'L0_attn_Dp': (1.0, 0.6),
     'L0_xattn_bq1': (0.0, 2.0),
     'L0_xattn_bk1': (0.0, 2.0),
     'L0_xattn_bv1': (0.0, 2.0),
     'L0_xattn_bo1': (0.0, 0.8),
     'L0_xattn_bq2': (0.0, 2.0),
     'L0_xattn_bk2': (0.0, 2.0),
     'L0_xattn_bv2': (0.0, 0.502),
     'L0_xattn_bo2': (0.0, 0.519),
     'L0_ffn_br': (0.0, 0.477),
     'L0_ffn_b1': (0.0, 2.0),
     'L0_ffn_b2': (0.0, 0.8)}
    factors = {'L0_attn_W_in': 7.014,
     'L0_attn_conv_w': 8.0,
     'L0_attn_W_xproj': 8.0,
     'L0_attn_W_dt': 8.0,
     'L0_attn_A_log': 8.0,
     'L0_attn_W_out': 7.331,
     'L0_xattn_Wq1': 8.0,
     'L0_xattn_Wk1': 7.167,
     'L0_xattn_Wv1': 4.862,
     'L0_xattn_Wo1': 4.158,
     'L0_xattn_Wq2': 3.898,
     'L0_xattn_Wk2': 3.409}
    for name, (base, spread) in spreads.items():
        noise = np.random.default_rng([zlib.crc32(name.encode()), seed]).standard_normal(out[name].shape)
        drawn = base * np.exp(spread * noise) if base else spread * noise
        out[name] = jnp.asarray(drawn.astype(out[name].dtype))
    for name, factor in factors.items():
        out[name] = (out[name] * factor).astype(out[name].dtype)
    return out
```

```python
from contextlib import ExitStack

import concourse.bass as bass
from concourse import mybir

FP32 = mybir.dt.float32
BF16 = mybir.dt.bfloat16
ALU = mybir.AluOpType
ACT = mybir.ActivationFunctionType
AX = mybir.AxisListType

P = 128
B, L, D = 4, 512, 128
T = L // P
DI, DT = 256, 2
RING = 3
N = 16
RANK = 64
CONV = 4
H, HD = 16, 8
SK, SKP = 154, 160
TAIL = SKP - P
PARTS = 3
PROD = PARTS * PARTS * HD
AUG = 96
KAUG = AUG + PARTS
GH = 4
E, FF = 8, 512
FC = FF // P
FIRST, REST = 9, 51
POOL_ONCE, DVE_ONCE = 33, 9
M_CONV, M_BC, M_DT, M_YZ = 20, 25, 28, 32
A_STAT, A_XN, A_V1, A_NM, A_V2 = 9, 13, 17, (21, 34), 30
F_STAT, F_XN, F_LOGITS, F_WT, F_ACC = 48, 52, 55, 62, 63
SCALE = float(HD) ** -0.5
NEG = -3.0e38
EPS = 1e-5
PT_HEADS = 6
CAUSAL = sum((L - P * j) for j in range(T))
PT_AT = [0, 512, 1024, 896]
PT_UNITS = [(0, 512, [0]), (512, 512, [1, 3]), (1024, 256, [2])]


class Signal:

    def __init__(self, nc, ctx, name, per_batch):
        self.name, self.per_batch = name, per_batch
        self.sem = ctx.enter_context(nc.semaphore(name))
        self.seen = 0
        self.here = 0

    def start(self, b):
        self.here = 0

    def at(self, b, k):
        return b * self.per_batch + k

    def by(self, instruction, amount=1):
        instruction.then_inc(self.sem, amount)
        self.seen += amount
        self.here += amount

    def settle(self, engine, b, but=0):
        engine.wait_ge(self.sem, self.at(b, self.here - but))


def interleave(ahead, behind):
    order, taken = [], 0
    for n, step in enumerate(ahead):
        order.append(step)
        upto = (n + 1) * len(behind) // len(ahead)
        order += behind[taken:upto]
        taken = upto
    return order


def decoder_kernel(nc, x, ctx_tokens, W_in, conv_w, conv_b, W_xproj, W_dt, b_dt, A_log, Dp, W_out,
                   Wq1, bq1, Wk1, bk1, Wv1, bv1, Wo1, bo1, Wq2, bq2, Wk2, bk2, Wv2, bv2, Wo2, bo2,
                   Wr, br, W1, b1, W2, b2, q_scratch, k_scratch, out):
    ctx = ExitStack()
    with ctx:
        def sb(name, shape, dt=FP32):
            return ctx.enter_context(nc.sbuf_tensor(name, shape, dt))

        signals = []

        def sig(name, per_batch):
            signals.append(Signal(nc, ctx, name, per_batch))
            return signals[-1]

        def once(name):
            return ctx.enter_context(nc.semaphore(name))

        w_in = sb("w_in", [P, 2 * DI])
        w_xp = sb("w_xp", [P, DT, AUG])
        w_bc = sb("w_bc", [P, DT, PARTS, 2 * N])
        w_dt = sb("w_dt", [AUG, DI])
        w_out = sb("w_out", [P, DT, D])
        cw = sb("cw", [P, DT, CONV])
        cb = sb("cb", [P, DT])
        bdt = sb("bdt", [P, DT])
        a_neg = sb("a_neg", [P, DT, N])
        a_log = sb("a_log", [P, DT, N])
        dp = sb("dp", [P, DT])
        wq, wk, wv, wo = ([sb(f"w{c}{i}", [P, D]) for i in (1, 2)] for c in "qkvo")
        bq, bk, bocol = ([sb(f"b{c}{i}", [P, 1]) for i in (1, 2)] for c in ("q", "k", "oc"))
        bvrow = [sb(f"bv{i}r", [P, D]) for i in (1, 2)]
        bo2row = sb("bo2r", [P, D])
        wr = sb("wr", [P, E])
        brrow = sb("brr", [P, E])
        w1 = sb("w1", [P, E, FF])
        w2 = sb("w2", [P, E, FC, D])
        b1c = sb("b1c", [P, E, FC])
        b2r = sb("b2r", [E, D])

        ident = sb("ident", [P, P])
        identb = sb("identb", [P, P], BF16)
        mask_q = sb("mask_q", [P, P], BF16)
        mask_k = sb("mask_k", [P, P], BF16)
        select = sb("select", [AUG, 2 * N, P], BF16)
        eps = sb("eps", [P, 1])
        prefer = sb("prefer", [P, E])

        x_tok = sb("x_tok", [P, T, D])
        mst = sb("mst", [P, T, 6])
        mmv = sb("mmv", [P, T, 2])
        mrs = sb("mrs", [P, T])
        mxn = sb("mxn", [P, T, D])
        xin = sb("xin", [P, DT, CONV - 1 + L])
        conv = sb("conv", [P, DT, L])
        sz = sb("sz", [P, DT, L])
        xc = sb("xc", [P, DT, L])
        bcs = sb("bcs", [AUG, L], BF16)
        bcm = sb("bcm", [AUG, L], BF16)
        spa = conv
        dts = sb("dts", [P, DT, L])
        u = sb("u", [P, DT, L])
        mxnT = u[:, 0, :]
        dA = sb("dA", [P, 2, DT, L])
        st = sb("st", [P, RING, DT, L])
        xdbl = st[0:AUG, RING - 1, 0, :]
        bcr = st[0:AUG, RING - 1, 1, :]
        yz = conv
        x1m = sb("x1m", [P, T, D])

        x1 = sb("x1", [P, T, D])
        ast = sb("ast", [P, T, 6])
        amv = sb("amv", [P, T, 2])
        ars = sb("ars", [P, T])
        axn = sb("axn", [P, T, D])
        axnT = sb("axnT", [P, L])
        ctok = sb("ctok", [P, 2, D])
        ctxT = sb("ctxT", [P, P])
        ctx4 = sb("ctx4", [P, GH, TAIL])
        ot = sb("ot", [P, GH, L])
        qp = ot[:, 0:3, :].bitcast(BF16).rearrange("p a (b t) -> p (a b) t", t=L).rearrange("p (i j) t -> p i j t", i=2)
        wteT = ot[0:E, 3, :]
        q_stack = sb("q_stack", [P, H, L], BF16)
        k_stack = sb("k_stack", [P, H, L], BF16)
        k2_stack = sb("k2_stack", [P, H, SKP], BF16)
        v1a = sb("v1a", [P, T, H, 32])
        v2a = sb("v2a", [P, H, 32])
        v2b = sb("v2b", [P, H, 32])
        negm = sb("negm", [P, T, H])
        nmr = sb("nmr", [P, T, H])
        nmp = sb("nmp", [P, T, PARTS, H], BF16)
        nmT = sb("nmT", [PARTS * H, L], BF16)
        pt = sb("pt", [P, PT_HEADS * CAUSAL])
        pth = pt[:, :].rearrange("p (s c) -> p s c", s=PT_HEADS)
        qf = pt[:, 0:2 * L].rearrange("p (i t) -> p i t", i=2)
        qr = pt[:, 2 * L:4 * L].rearrange("p (i t) -> p i t", i=2)
        h1 = pt[:, 0:2 * FC * L].rearrange("p (r f t) -> p r f t", r=2, f=FC)
        orc = sb("orc", [P, T, H])
        otok = axn
        oT = axn[:, :, :].rearrange("p t d -> p (t d)")
        hT = axnT
        x2 = x1
        lg = sb("lg", [P, T, E])
        lmx = sb("lmx", [P, T])
        lex = sb("lex", [P, T, E])
        lsm = sb("lsm", [P, T])
        gate = sb("gate", [P, T])
        oneh = sb("oneh", [P, T, E])
        wte = sb("wte", [P, T, E])
        acc = sb("acc", [P, T, D])

        def cross(g, n):
            at = ((GH + 1) * (g % 2) + n) * L
            return pt[:, at:at + L]

        ps = ctx.enter_context(nc.psum_tensor("ps", [P, 8, 512], FP32))

        loaded = once("loaded")
        loaded_rest = once("loaded_rest")
        pool_once = once("pool_once")
        dve_once = once("dve_once")
        act_once = once("act_once")
        turned = once("turned")

        x_in = sig("x_in", 16)
        m_dve = sig("m_dve", M_YZ)
        m_rstd = sig("m_rstd", 2)
        m_xnt_ps = sig("m_xnt_ps", 1)
        m_xnt = sig("m_xnt", 1)
        m_xz = sig("m_xz", 4)
        m_xin = sig("m_xin", 2)
        m_silu = sig("m_silu", 2)
        m_xp_ps = sig("m_xp_ps", 2)
        m_xdbl = sig("m_xdbl", 1)
        m_dt_ps = sig("m_dt_ps", 2)
        m_soft = sig("m_soft", 4)
        b_bc = sig("b_bc", N)
        c_bc = sig("c_bc", N)
        decay = sig("decay", N)
        driven = sig("driven", N)
        scanned = sig("scanned", 2 * N)
        weighed = sig("weighed", N)
        summed = sig("summed", N)
        m_out_ps = sig("m_out_ps", 1)
        m_x1 = sig("m_x1", 1)

        ctx_in = sig("ctx_in", 32)
        a_dve = sig("a_dve", F_ACC)
        a_rstd = sig("a_rstd", 2)
        a_xnt_ps = sig("a_xnt_ps", 1)
        a_xnt = sig("a_xnt", 1)
        qk_ps = sig("qk_ps", 4)
        v_ps = sig("v_ps", 2)
        qk_act = sig("qk_act", 12)
        qk_parts = sig("qk_parts", 8)
        spilled = sig("spilled", 64)
        stacked = sig("stacked", 256)
        s_max_ps = sig("s_max_ps", 22 + 12)
        s_max = sig("s_max", 22 + 12)
        nm_ps = sig("nm_ps", 2)
        nm_sb = sig("nm_sb", 2)
        nm_in = sig("nm_in", 96)
        sc_ps = sig("sc_ps", 3 * H + 5 * H // GH)
        probs = sig("probs", 3 * H + 5 * H // GH)
        pv_ps = sig("pv_ps", 2 * H // GH)
        pv_sb = sig("pv_sb", 2 * H // GH)
        ot_ps = sig("ot_ps", 2 * T)
        o_tok = sig("o_tok", 2 * T)
        oT_ps = sig("oT_ps", 2)
        oT_sb = sig("oT_sb", 2)
        hT_ps = sig("hT_ps", 1)
        hT_sb = sig("hT_sb", 1)
        ct_ps = sig("ct_ps", 1)
        ct_sb = sig("ct_sb", 2)
        o2_ps = sig("o2_ps", 1)
        f_rstd = sig("f_rstd", 2)
        f_xnt_ps = sig("f_xnt_ps", 1)
        f_xnt = sig("f_xnt", 1)
        lg_ps = sig("lg_ps", 1)
        lg_exp = sig("lg_exp", 1)
        wt_ps = sig("wt_ps", 1)
        wt_sb = sig("wt_sb", 1)
        b2_ps = sig("b2_ps", 1)
        h1_ps = sig("h1_ps", E * FC)
        h1_act = sig("h1_act", E * FC // 2)
        h1_dve = sig("h1_dve", E * FC // 2)
        ye_ps = sig("ye_ps", E)
        ye_acc = sig("ye_acc", E)
        stored = sig("stored", 16)

        SELF_MAX = []
        for i in range(T):
            per_bank = L // (P * (i + 1))
            SELF_MAX += [(i, h0, per_bank) for h0 in range(0, H, 2 * per_bank)]
        CROSS_MAX = [(i, h0, min(6, H - h0)) for i in range(T) for h0 in (0, 6, 12)]

        MAMBA = [("m_norm", 0), ("m_in", 0), ("m_conv", 0), ("m_proj", 0), ("m_soft", 0)]
        MAMBA += [("scan", n) for n in range(N)] + [("m_out", 0)]
        AFTER = [("a_norm", 0), ("qkv", 0), ("stack", 0)]
        AFTER += [("smax", g) for g in range(len(SELF_MAX))] + [("negm", 0)]
        AFTER += [("exp", h) for h in range(H)] + [("pv", H // GH - 1)]
        AFTER += [("o_norm", 0), ("q2", 0), ("stack", 1)]
        AFTER += [("cmax", g) for g in range(len(CROSS_MAX))] + [("negm", 1)]
        AFTER += [("cexp", g) for g in range(H // GH)] + [("cpv", H // GH - 1)]
        AFTER += [("o_norm", 1), ("f_norm", 0), ("route", 0)]
        AFTER += [("expert", e) for e in range(E)] + [("ye", E - 1), ("store", 0)]

        def walk(steps):
            for name, k in MAMBA:
                if name in steps:
                    steps[name](0, k)
            for b in range(B - 1):
                for (name, k) in interleave(MAMBA, AFTER):
                    if name in steps:
                        steps[name](b + 1 if (name, k) in MAMBA else b, k)
            for name, k in AFTER:
                if name in steps:
                    steps[name](B - 1, k)

        ctx.enter_context(nc.allow_non_contiguous_dma(reason="biases go to partitions once"))
        block = ctx.enter_context(nc.Block())

        @block.sync
        def _(sp):
            first = [
                (w_in[:, :], W_in), (w_xp[:, :, :], W_xproj.rearrange("(d p) e -> p d e", p=P)),
                (w_dt[0:RANK, :], W_dt), (w_out[:, :, :], W_out.rearrange("(d p) e -> p d e", p=P)),
                (cw[:, :, :], conv_w.rearrange("(d p) k -> p d k", p=P)),
                (cb[:, :], conv_b.rearrange("(d p) -> p d", p=P)),
                (bdt[:, :], b_dt.rearrange("(d p) -> p d", p=P)),
                (a_log[:, :, :], A_log.rearrange("(d p) n -> p d n", p=P)),
                (dp[:, :], Dp.rearrange("(d p) -> p d", p=P)),
            ]
            rest = []
            for i, (q, k, v, o) in enumerate([(Wq1, Wk1, Wv1, Wo1), (Wq2, Wk2, Wv2, Wo2)]):
                for to, w in ((acc[:, 2 * i, :], q), (acc[:, 2 * i + 1, :], k), (wv[i][:, :], v)):
                    rest.append((to.rearrange("d (h e) -> d h e", h=H), w.rearrange("h d e -> d h e")))
                rest.append((wo[i][:, :], o))
            for i, (q, k, v, o) in enumerate([(bq1, bk1, bv1, bo1), (bq2, bk2, bv2, bo2)]):
                for e in range(HD):
                    rest.append((bq[i][e * H:(e + 1) * H, :], q[:, e:e + 1]))
                    rest.append((bk[i][e * H:(e + 1) * H, :], k[:, e:e + 1]))
                rest.append((bvrow[i][:, :], v.rearrange("h e -> (h e)").partition_broadcast(P)))
                rest.append((bocol[i][:, :], o.rearrange("(e o) -> e o", o=1)))
            rest += [
                (bo2row[:, :], bo2.partition_broadcast(P)), (wr[:, :], Wr), (brrow[:, :], br.partition_broadcast(P)),
                (w1[:, :, :], W1.rearrange("e h f -> h e f")),
                (w2[:, :, :, :], W2.rearrange("e (c p) h -> p e c h", p=P)),
                (b1c[:, :, :], b1.rearrange("e (c p) -> p e c", p=P)), (b2r[:, :], b2),
            ]
            assert len(first) == FIRST and len(rest) == REST

            def m_norm(b, _):
                sp.wait_ge(m_x1.sem, m_x1.at(b, 0))
                x_in.by(sp.dma_start(x_tok[:, :, :], x[b].rearrange("(t p) d -> p t d", p=P)), 16)
                if b == 0:
                    for to, src in rest:
                        sp.dma_start(to, src).then_inc(loaded_rest, 16)

            def a_norm(b, _):
                sp.wait_ge(ct_ps.sem, ct_ps.at(b, 0))
                ctx_in.by(sp.dma_start(ctok[:, 0, :], ctx_tokens[b, 0:P, :]), 16)
                ctx_in.by(sp.dma_start(ctok[0:SK - P, 1, :], ctx_tokens[b, P:SK, :]), 16)

            def stack(b, a):
                width, ks = ((L, k_stack), (SK, k2_stack))[a]
                q_of = q_scratch.rearrange("j (e h) t -> (j e) h t", h=H)
                k_of = k_scratch.rearrange("j (e h) t -> (j e) h t", h=H)[:, :, 0:width]
                sp.wait_ge(qk_parts.sem, qk_parts.at(b, 4 * a + 3))
                spilled.by(sp.dma_start(q_scratch.rearrange("j r t -> r j t"), qp[:, 0, :, :]), 16)
                sp.wait_ge(qk_parts.sem, qk_parts.at(b, 4 * a + 4))
                spilled.by(sp.dma_start(k_scratch[:, :, 0:width].rearrange("j r t -> r j t"), qp[:, 1, :, 0:width]), 16)
                sp.wait_ge(sc_ps.sem, sc_ps.at(b, 3 * H * a))
                sp.wait_ge(spilled.sem, spilled.at(b, 32 * a + 32))
                rows = PARTS * HD
                for rep in range(PARTS):
                    at, turn, cut = rep * rows, rep * HD, (PARTS - rep) * HD
                    stacked.by(sp.dma_start(q_stack[at:at + rows, :, :], q_of), 16)
                    stacked.by(sp.dma_start(ks[at:at + cut, :, 0:width], k_of[turn:rows]), 16)
                    if rep:
                        stacked.by(sp.dma_start(ks[at + cut:at + rows, :, 0:width], k_of[0:turn]), 16)
                sp.wait_ge(stacked.sem, stacked.at(b, 128 * (a + 1)))

            def negm_rows(b, a):
                sp.wait_ge(nm_sb.sem, nm_sb.at(b, a + 1))
                for j in range(PARTS):
                    nm_in.by(sp.dma_start(q_stack[AUG + j:AUG + j + 1, :, :], nmT[j * H:(j + 1) * H, :]), 16)

            def store(b, _):
                sp.wait_ge(ye_acc.sem, ye_acc.at(b, E))
                stored.by(sp.dma_start(out[b].rearrange("(t p) d -> p t d", p=P), acc[:, :, :]), 16)

            for to, src in first:
                sp.dma_start(to, src).then_inc(loaded, 16)
            walk({"m_norm": m_norm, "a_norm": a_norm, "stack": stack, "negm": negm_rows, "store": store})
            sp.wait_ge(stored.sem, stored.at(B, 0))

        @block.gpsimd
        def _(pool):
            pool.memset(ident[:, :], 0.0).then_inc(pool_once, 1)
            pool.memset(mask_q[:, :], 0.0).then_inc(pool_once, 1)
            pool.memset(mask_k[:, :], 0.0).then_inc(pool_once, 1)
            pool.memset(select[:, :, :], 0.0).then_inc(pool_once, 1)
            pool.wait_ge(pool_once, 4)
            pool.affine_select(out=ident[:, :], in_=ident[:, :], compare_op=ALU.not_equal, fill=1.0,
                               base=0, pattern=[[-1, P]], channel_multiplier=1).then_inc(pool_once, 1)
            pool.affine_select(out=mask_q[:, :], in_=mask_q[:, :], compare_op=ALU.is_ge, fill=NEG,
                               base=0, pattern=[[-1, P]], channel_multiplier=1).then_inc(pool_once, 1)
            pool.affine_select(out=mask_k[:, :], in_=mask_k[:, :], compare_op=ALU.is_ge, fill=NEG,
                               base=0, pattern=[[1, P]], channel_multiplier=-1).then_inc(pool_once, 1)
            for j in range(PARTS):
                pool.affine_select(out=select[:, :, :], in_=select[:, :, :], compare_op=ALU.not_equal, fill=1.0,
                                   base=-2 * N * j, pattern=[[-1, 2 * N], [0, P]], channel_multiplier=1).then_inc(pool_once, 1)
                pool.wait_ge(pool_once, 8 + j)
            for e in range(E):
                pool.memset(prefer[:, e:e + 1], float(E - e)).then_inc(pool_once, 1)
            for view in (v1a, v2a, v2b, q_stack, k_stack, k2_stack):
                pool.memset(view[(slice(None),) * len(view.shape)], 0.0).then_inc(pool_once, 1)
            pool.memset(ctx4[:, :, :], 0.0).then_inc(pool_once, 1)
            pool.wait_ge(pool_once, 25)
            ones = [v1a[:, :, :, HD:HD + 1], v2a[:, :, HD:HD + 1]]
            ones += [v2b[32 * c:32 * c + SK - P, :, :].rearrange("p (g c) x -> p g c x", c=GH)[:, :, c, HD:HD + 1] for c in range(GH)]
            ones += [k_stack[AUG:P, :, :], k2_stack[AUG:P, :, 0:SK]]
            for n, view in enumerate(ones):
                pool.memset(view, 1.0).then_inc(pool_once, 1)
                pool.wait_ge(pool_once, 26 + n)

            def split(b, a):
                width = (L, SK)[a]
                if b == 0 and a == 0:
                    pool.wait_ge(loaded_rest, REST * 16)
                    for i, to in enumerate((wq[0], wk[0], wq[1], wk[1])):
                        pool.tensor_copy(to[:, :].rearrange("d (e h) -> d h e", h=H),
                                         acc[:, i, :].rearrange("d (h e) -> d h e", h=H)).then_inc(turned, 1)
                for i, w in ((0, L), (1, width)):
                    pool.wait_ge(qk_act.sem, qk_act.at(b, 6 * a + 2 * i + 2))
                    pool.wait_ge(qk_parts.sem, qk_parts.at(b, 4 * a))
                    qk_parts.by(pool.tensor_tensor(qr[:, i, 0:w], qf[:, i, 0:w], qp[:, i, 0, 0:w], ALU.subtract))
                for i, w in ((0, L), (1, width)):
                    pool.wait_ge(qk_act.sem, qk_act.at(b, 6 * a + 5 + i))
                    qk_parts.by(pool.tensor_tensor(qp[:, i, 2, 0:w], qr[:, i, 0:w], qp[:, i, 1, 0:w], ALU.subtract))

            walk({"qkv": lambda b, _: split(b, 0), "q2": lambda b, _: split(b, 1)})

        @block.scalar
        def _(act):
            act.wait_ge(loaded, FIRST * 16)
            nc.scalar.activation(a_neg[:, :, :], a_log[:, :, :], ACT.Exp).then_inc(act_once, 1)
            act.wait_ge(dve_once, DVE_ONCE)
            act.wait_ge(pool_once, POOL_ONCE)

            def rstd(b, sig, mv, rs, have, at):
                act.wait_ge(have.sem, have.at(b, at))
                sig.by(nc.scalar.activation(rs[:, :], mv[:, :, 1], ACT.Ln, bias=eps[:, 0:1]))
                act.wait_ge(sig.sem, sig.at(b, 1))
                sig.by(nc.scalar.activation(rs[:, :], rs[:, :], ACT.Exp, scale=-0.5))

            def m_norm(b, _):
                rstd(b, m_rstd, mmv, mrs, m_dve, 2 * T)
                act.wait_ge(m_xnt_ps.sem, m_xnt_ps.at(b, 1))
                m_xnt.by(nc.scalar.copy(mxnT[:, :], ps[:, 2, :]))

            def m_in(b, _):
                for d in range(DT):
                    act.wait_ge(m_xz.sem, m_xz.at(b, d + 1))
                    m_xin.by(nc.scalar.copy(xin[:, d, CONV - 1:], ps[:, d, :]))

            def m_conv(b, _):
                act.wait_ge(m_xz.sem, m_xz.at(b, 4))
                act.wait_ge(m_dve.sem, m_dve.at(b, 0))
                m_silu.by(nc.scalar.activation(sz[:, :, :], ps[:, 2:4, :], ACT.Silu))
                act.wait_ge(m_dve.sem, m_dve.at(b, M_CONV))
                m_silu.by(nc.scalar.activation(xc[:, :, :], conv[:, :, :], ACT.Silu))

            def m_proj(b, _):
                act.wait_ge(m_xp_ps.sem, m_xp_ps.at(b, 1))
                m_xdbl.by(nc.scalar.copy(xdbl[:, :], ps[0:AUG, 0, :]))

            def m_softplus(b, _):
                for d in range(DT):
                    act.wait_ge(m_dt_ps.sem, m_dt_ps.at(b, d + 1))
                    m_soft.by(nc.scalar.activation(spa[:, d, :], ps[:, 2 + d, :], ACT.Abs, bias=bdt[:, d:d + 1]))
                act.wait_ge(m_soft.sem, m_soft.at(b, 2))
                m_soft.by(nc.scalar.activation(spa[:, :, :], spa[:, :, :], ACT.Exp, scale=-1.0))
                act.wait_ge(m_soft.sem, m_soft.at(b, 3))
                m_soft.by(nc.scalar.activation(spa[:, :, :], spa[:, :, :], ACT.Ln, bias=1.0))

            def scan(b, n):
                if n == 0:
                    act.wait_ge(m_dve.sem, m_dve.at(b, M_DT))
                act.wait_ge(scanned.sem, scanned.at(b, max(DT * (n - 1), 0)))
                for d in range(DT):
                    last = nc.scalar.activation(dA[:, n % 2, d, 1:], dts[:, d, 1:], ACT.Exp, scale=a_neg[:, d, n:n + 1])
                decay.by(last)

            def a_norm(b, _):
                rstd(b, a_rstd, amv, ars, a_dve, A_STAT)
                act.wait_ge(a_xnt_ps.sem, a_xnt_ps.at(b, 1))
                a_xnt.by(nc.scalar.copy(axnT[:, :], ps[:, 4, :]))
                act.wait_ge(ct_ps.sem, ct_ps.at(b, 1))
                ct_sb.by(nc.scalar.copy(ctxT[:, :], ps[:, 5, 0:P]))
                ct_sb.by(nc.scalar.copy(ctx4[:, :, 0:SK - P], ps[:, 5, P:SK].unsqueeze(1).to_broadcast([P, GH, SK - P])))

            def split(b, a):
                width = (L, SK)[a]
                if b == 0 and a == 0:
                    act.wait_ge(loaded_rest, REST * 16)
                for i, (w, bias) in enumerate(((L, bq[a]), (width, bk[a]))):
                    act.wait_ge(qk_ps.sem, qk_ps.at(b, 2 * a + i + 1))
                    act.wait_ge(qk_parts.sem, qk_parts.at(b, 4 * a))
                    qk_act.by(nc.scalar.activation(qf[:, i, 0:w], ps[:, 6 + i, 0:w], ACT.Identity, bias=bias[:, 0:1]))
                    act.wait_ge(spilled.sem, spilled.at(b, 32 * a))
                    qk_act.by(nc.scalar.activation(qp[:, i, 0, 0:w], ps[:, 6 + i, 0:w], ACT.Identity, bias=bias[:, 0:1]))
                for i, w in enumerate((L, width)):
                    act.wait_ge(qk_parts.sem, qk_parts.at(b, 4 * a + i + 1))
                    qk_act.by(nc.scalar.copy(qp[:, i, 1, 0:w], qr[:, i, 0:w]))

            def negm_rows(b, a):
                act.wait_ge(nm_ps.sem, nm_ps.at(b, a + 1))
                act.wait_ge(nm_in.sem, nm_in.at(b, 48 * a))
                nm_sb.by(nc.scalar.copy(nmT[:, :], ps[0:PARTS * H, 4, :]))

            def exp(b, h):
                act.wait_ge(pv_ps.sem, pv_ps.at(b, (h - PT_HEADS) // GH + 1 if h >= PT_HEADS else 0))
                for n, (at, w, _) in enumerate(PT_UNITS):
                    r = 3 * h + n
                    act.wait_ge(sc_ps.sem, sc_ps.at(b, r + 1))
                    probs.by(nc.scalar.activation(pth[:, h % PT_HEADS, at:at + w], ps[:, 4 + r % 3, 0:w], ACT.Exp, scale=SCALE))

            def cexp(b, g):
                act.wait_ge(pv_ps.sem, pv_ps.at(b, H // GH + g - 1))
                for n in range(GH + 1):
                    r = 3 * H + (GH + 1) * g + n
                    to = cross(g, n)
                    act.wait_ge(sc_ps.sem, sc_ps.at(b, r + 1))
                    probs.by(nc.scalar.activation(to, ps[:, 4 + r % 3, :], ACT.Exp, scale=SCALE))

            def o_norm(b, a):
                act.wait_ge(oT_ps.sem, oT_ps.at(b, a + 1))
                oT_sb.by(nc.scalar.copy(oT[:, :], ps[:, 4, :]))

            def q2(b, _):
                act.wait_ge(hT_ps.sem, hT_ps.at(b, 1))
                hT_sb.by(nc.scalar.activation(hT[:, :], ps[:, 5, :], ACT.Identity, bias=bocol[0][:, 0:1]))
                split(b, 1)

            def f_norm(b, _):
                rstd(b, f_rstd, amv, ars, a_dve, F_STAT)
                act.wait_ge(f_xnt_ps.sem, f_xnt_ps.at(b, 1))
                f_xnt.by(nc.scalar.copy(axnT[:, :], ps[:, 4, :]))

            def route(b, _):
                act.wait_ge(a_dve.sem, a_dve.at(b, F_LOGITS))
                lg_exp.by(nc.scalar.activation(lex[:, :, :], lg[:, :, :], ACT.Exp))
                act.wait_ge(wt_ps.sem, wt_ps.at(b, 1))
                wt_sb.by(nc.scalar.copy(wteT[:, :], ps[0:E, 7, :]))

            def expert(b, e):
                act.wait_ge(ye_ps.sem, ye_ps.at(b, max(e - 1, 0)))
                for f in range(0, FC, 2):
                    act.wait_ge(h1_ps.sem, h1_ps.at(b, FC * e + f + 1))
                    h1_act.by(nc.scalar.activation(h1[:, e % 2, f, :], ps[:, 4, :], ACT.Relu, bias=b1c[:, e, f:f + 1]))

            walk({"m_norm": m_norm, "m_in": m_in, "m_conv": m_conv, "m_proj": m_proj, "m_soft": m_softplus, "scan": scan,
                  "a_norm": a_norm, "qkv": lambda b, _: split(b, 0), "negm": negm_rows, "exp": exp, "o_norm": o_norm,
                  "q2": q2, "cexp": cexp, "f_norm": f_norm, "route": route, "expert": expert})

        @block.vector
        def _(dve):
            nc.vector.memset(eps[:, :], EPS).then_inc(dve_once, 1)
            nc.vector.memset(dA[:, :, :, 0:1], 0.0).then_inc(dve_once, 1)
            nc.vector.memset(xin[:, :, 0:CONV - 1], 0.0).then_inc(dve_once, 1)
            nc.vector.memset(w_dt[RANK:AUG, :], 0.0).then_inc(dve_once, 1)
            dve.wait_ge(pool_once, POOL_ONCE)
            nc.vector.tensor_copy(identb[:, :], ident[:, :]).then_inc(dve_once, 1)
            dve.wait_ge(loaded, FIRST * 16)
            for j in range(PARTS):
                nc.vector.tensor_copy(w_bc[:, :, j, :], w_xp[:, :, RANK:AUG]).then_inc(dve_once, 1)
            dve.wait_ge(act_once, 1)
            nc.vector.tensor_scalar(a_neg[:, :, :], a_neg[:, :, :], -1.0, None, ALU.mult).then_inc(dve_once, 1)
            dve.wait_ge(dve_once, DVE_ONCE)

            def norm_stats(b, sig, src, st, mv):
                for t in range(T):
                    sig.by(nc.vector.bn_stats(st[:, t, :], src[:, t, :]))
                sig.settle(dve, b)
                for t in range(T):
                    sig.by(nc.vector.bn_aggr(mv[:, t, :], st[:, t, :]))
                sig.settle(dve, b)

            def norm_scale(b, sig, have, src, mv, rs, to):
                dve.wait_ge(have.sem, have.at(b, 2))
                for t in range(T):
                    sig.by(nc.vector.tensor_scalar(to[:, t, :], src[:, t, :], mv[:, t, 0:1], rs[:, t:t + 1],
                                                   ALU.subtract, ALU.mult))

            def m_norm(b, _):
                m_dve.start(b)
                dve.wait_ge(x_in.sem, x_in.at(b, 16))
                norm_stats(b, m_dve, x_tok, mst, mmv)
                norm_scale(b, m_dve, m_rstd, x_tok, mmv, mrs, mxn)

            def m_conv(b, _):
                for d in range(DT):
                    dve.wait_ge(m_xin.sem, m_xin.at(b, d + 1))
                    m_dve.by(nc.vector.tensor_scalar(conv[:, d, :], xin[:, d, 0:L], cw[:, d, 0:1], cb[:, d:d + 1],
                                                     ALU.mult, ALU.add))
                for k in range(1, CONV):
                    for d in range(DT):
                        m_dve.settle(dve, b, 1)
                        m_dve.by(nc.vector.scalar_tensor_tensor(out=conv[:, d, :], in0=xin[:, d, k:k + L],
                                                                scalar=cw[:, d, k:k + 1], in1=conv[:, d, :],
                                                                op0=ALU.mult, op1=ALU.add))
                assert m_dve.here == M_CONV

            def m_proj(b, _):
                dve.wait_ge(m_xp_ps.sem, m_xp_ps.at(b, 2))
                m_dve.by(nc.vector.tensor_copy(bcs[:, :], ps[0:AUG, 1, :]))
                m_dve.settle(dve, b)
                m_dve.by(nc.vector.tensor_tensor(bcr[:, :], ps[0:AUG, 1, :], bcs[:, :], ALU.subtract))
                m_dve.settle(dve, b)
                m_dve.by(nc.vector.tensor_copy(bcs[32:64, :], bcr[32:64, :]))
                m_dve.by(nc.vector.tensor_copy(bcm[64:96, :], bcr[64:96, :]))
                m_dve.settle(dve, b)
                m_dve.by(nc.vector.tensor_tensor(bcs[64:96, :], bcr[64:96, :], bcm[64:96, :], ALU.subtract))
                assert m_dve.here == M_BC

            def m_softplus(b, _):
                for d in range(DT):
                    dve.wait_ge(m_soft.sem, m_soft.at(b, d + 1))
                    m_dve.by(nc.vector.tensor_scalar(dts[:, d, :], ps[:, 2 + d, :], bdt[:, d:d + 1], 0.0, ALU.add, ALU.max))
                dve.wait_ge(m_soft.sem, m_soft.at(b, 4))
                m_dve.settle(dve, b)
                m_dve.by(nc.vector.tensor_tensor(dts[:, :, :], dts[:, :, :], spa[:, :, :], ALU.add))
                assert m_dve.here == M_DT
                m_dve.settle(dve, b)
                dve.wait_ge(m_silu.sem, m_silu.at(b, 2))
                m_dve.by(nc.vector.tensor_tensor(u[:, :, :], dts[:, :, :], xc[:, :, :], ALU.mult))
                m_dve.settle(dve, b)
                drive(b, 0)

            def drive(b, n):
                dve.wait_ge(b_bc.sem, b_bc.at(b, n + 1))
                dve.wait_ge(summed.sem, summed.at(b, max(n - RING + 1, 0)))
                driven.by(nc.vector.tensor_tensor(st[:, n % RING, :, :], u[:, :, :],
                                                  ps[:, 2, :].unsqueeze(1).to_broadcast([P, DT, L]), ALU.mult))

            def scan(b, n):
                dve.wait_ge(decay.sem, decay.at(b, n + 1))
                dve.wait_ge(driven.sem, driven.at(b, n + 1))
                for d in range(DT):
                    scanned.by(nc.vector.tensor_tensor_scan(st[:, n % RING, d, :], dA[:, n % 2, d, :], st[:, n % RING, d, :],
                                                            0.0, ALU.mult, ALU.add))
                if n + 1 < N:
                    drive(b, n + 1)
                dve.wait_ge(c_bc.sem, c_bc.at(b, n + 1))
                dve.wait_ge(scanned.sem, scanned.at(b, DT * (n + 1)))
                weighed.by(nc.vector.tensor_tensor(st[:, n % RING, :, :], st[:, n % RING, :, :],
                                                   ps[:, 3, :].unsqueeze(1).to_broadcast([P, DT, L]), ALU.mult))

            def m_out(b, _):
                dve.wait_ge(summed.sem, summed.at(b, N))
                for d in range(DT):
                    m_dve.by(nc.vector.scalar_tensor_tensor(out=yz[:, d, :], in0=xc[:, d, :], scalar=dp[:, d:d + 1],
                                                            in1=ps[:, d, :], op0=ALU.mult, op1=ALU.add))
                dve.wait_ge(m_silu.sem, m_silu.at(b, 1))
                m_dve.settle(dve, b)
                m_dve.by(nc.vector.tensor_tensor(yz[:, :, :], yz[:, :, :], sz[:, :, :], ALU.mult))
                assert m_dve.here == M_YZ
                dve.wait_ge(m_out_ps.sem, m_out_ps.at(b, 1))
                if b:
                    dve.wait_ge(a_dve.sem, a_dve.at(b - 1, 1))
                m_x1.by(nc.vector.tensor_tensor(x1m[:, :, :], x_tok[:, :, :], ps[:, 2, :].rearrange("p (t d) -> p t d", t=T), ALU.add))

            def a_norm(b, _):
                a_dve.start(b)
                dve.wait_ge(m_x1.sem, m_x1.at(b, 1))
                a_dve.by(nc.vector.tensor_copy(x1[:, :, :], x1m[:, :, :]))
                a_dve.settle(dve, b)
                norm_stats(b, a_dve, x1, ast, amv)
                assert a_dve.here == A_STAT
                norm_scale(b, a_dve, a_rstd, x1, amv, ars, axn)
                assert a_dve.here == A_XN

            def qkv(b, _):
                if b == 0:
                    dve.wait_ge(loaded_rest, REST * 16)
                dve.wait_ge(v_ps.sem, v_ps.at(b, 1))
                dve.wait_ge(pv_ps.sem, pv_ps.at(b, 0))
                for t in range(T):
                    a_dve.by(nc.vector.tensor_tensor(v1a[:, t, :, 0:HD], ps[:, 4, t * P:(t + 1) * P].rearrange("p (h e) -> p h e", h=H),
                                                     bvrow[0][:, :].rearrange("p (h e) -> p h e", h=H), ALU.add))
                assert a_dve.here == A_V1

            def smax(b, g):
                i, h0, per = SELF_MAX[g]
                w = P * (i + 1)
                dve.wait_ge(s_max_ps.sem, s_max_ps.at(b, g + 1))
                bank = 4 + 2 * (g % 2)
                s_max.by(nc.vector.tensor_reduce(negm[:, i, h0:h0 + 2 * per].rearrange("p (a c) -> p a c", a=2),
                                                 ps[:, bank:bank + 2, 0:per * w].rearrange("p a (c k) -> p a c k", k=w),
                                                 AX.X, ALU.max, negate=True))

            def cmax(b, g):
                i, h0, n = CROSS_MAX[g]
                per = n // 2
                dve.wait_ge(s_max_ps.sem, s_max_ps.at(b, len(SELF_MAX) + g + 1))
                bank = 4 + 2 * (g % 2)
                s_max.by(nc.vector.tensor_reduce(negm[:, i, h0:h0 + n].rearrange("p (a c) -> p a c", a=2),
                                                 ps[:, bank:bank + 2, 0:per * SK].rearrange("p a (c k) -> p a c k", k=SK),
                                                 AX.X, ALU.max, negate=True))

            def negm_rows(b, a):
                dve.wait_ge(s_max.sem, s_max.at(b, (len(SELF_MAX), len(SELF_MAX) + len(CROSS_MAX))[a]))
                a_dve.by(nc.vector.tensor_copy(nmp[:, :, 0, :], negm[:, :, :]))
                a_dve.settle(dve, b)
                a_dve.by(nc.vector.tensor_tensor(nmr[:, :, :], negm[:, :, :], nmp[:, :, 0, :], ALU.subtract))
                a_dve.settle(dve, b)
                a_dve.by(nc.vector.tensor_copy(nmp[:, :, 1, :], nmr[:, :, :]))
                a_dve.settle(dve, b)
                a_dve.by(nc.vector.tensor_tensor(nmp[:, :, 2, :], nmr[:, :, :], nmp[:, :, 1, :], ALU.subtract))
                a_dve.settle(dve, b)
                assert a_dve.here == A_NM[a]

            def take_pv(b, a, g):
                n = a * (H // GH) + g
                dve.wait_ge(pv_ps.sem, pv_ps.at(b, n + 1))
                dve.wait_ge(ot_ps.sem, ot_ps.at(b, T * a))
                pv_sb.by(nc.vector.tensor_copy(ot[:, g, :], ps[:, 7, :]))

            def exp(b, h):
                if h % GH == 2 and h > GH:
                    take_pv(b, 0, h // GH - 1)

            def cexp(b, g):
                if g:
                    take_pv(b, 1, g - 1)

            def o_norm(b, a):
                for i in range(T):
                    dve.wait_ge(ot_ps.sem, ot_ps.at(b, T * a + i + 1))
                    o = ps[:, 4 + i, :].rearrange("p (h x) -> p h x", x=32)
                    a_dve.by(nc.vector.reciprocal(orc[:, i, :].unsqueeze(2), o[:, :, HD:HD + 1]))
                    a_dve.settle(dve, b)
                    o_tok.by(nc.vector.tensor_tensor(otok[:, i, :].rearrange("p (h e) -> p h e", h=H), o[:, :, 0:HD],
                                                     orc[:, i, :].unsqueeze(2).to_broadcast([P, H, HD]), ALU.mult))
                if a:
                    dve.wait_ge(o2_ps.sem, o2_ps.at(b, 1))
                    a_dve.by(nc.vector.tensor_tensor(x2[:, :, :], x1[:, :, :], ps[:, 5, :].rearrange("p (t d) -> p t d", t=T), ALU.add))
                    a_dve.settle(dve, b)
                    a_dve.by(nc.vector.tensor_tensor(x2[:, :, :], x2[:, :, :], bo2row[:, :].unsqueeze(1).to_broadcast([P, T, D]), ALU.add))
                    a_dve.settle(dve, b)

            def q2(b, _):
                dve.wait_ge(v_ps.sem, v_ps.at(b, 2))
                a_dve.by(nc.vector.tensor_tensor(v2a[:, :, 0:HD], ps[:, 4, 0:P].rearrange("p (h e) -> p h e", h=H),
                                                 bvrow[1][:, :].rearrange("p (h e) -> p h e", h=H), ALU.add))
                for c in range(GH):
                    rows = slice(32 * c, 32 * c + SK - P)
                    a_dve.by(nc.vector.tensor_tensor(
                        v2b[rows, :, :].rearrange("p (g c) x -> p g c x", c=GH)[:, :, c, 0:HD],
                        ps[rows, 4, P:2 * P].rearrange("p (g c e) -> p g c e", c=GH, e=HD)[:, :, c, :],
                        bvrow[1][rows, :].rearrange("p (g c e) -> p g c e", c=GH, e=HD)[:, :, c, :], ALU.add))
                a_dve.settle(dve, b)
                assert a_dve.here == A_V2

            def f_norm(b, _):
                norm_stats(b, a_dve, x2, ast, amv)
                assert a_dve.here == F_STAT
                norm_scale(b, a_dve, f_rstd, x2, amv, ars, axn)
                assert a_dve.here == F_XN

            def route(b, _):
                chain = lambda ins: (a_dve.by(ins), a_dve.settle(dve, b))
                wide = lambda col: col[:, :].unsqueeze(2).to_broadcast([P, T, E])
                row = lambda r: r[:, :].unsqueeze(1).to_broadcast([P, T, E])
                dve.wait_ge(lg_ps.sem, lg_ps.at(b, 1))
                chain(nc.vector.tensor_tensor(lg[:, :, :], ps[:, 6, 0:T * E].rearrange("p (t e) -> p t e", t=T), row(brrow), ALU.add))
                chain(nc.vector.tensor_reduce(lmx[:, :], lg[:, :, :], AX.X, ALU.max))
                chain(nc.vector.tensor_tensor(lg[:, :, :], lg[:, :, :], wide(lmx), ALU.subtract))
                assert a_dve.here == F_LOGITS
                chain(nc.vector.tensor_scalar(oneh[:, :, :], lg[:, :, :], 0.0, None, ALU.is_equal))
                chain(nc.vector.tensor_tensor(oneh[:, :, :], oneh[:, :, :], row(prefer), ALU.mult))
                chain(nc.vector.tensor_reduce(lmx[:, :], oneh[:, :, :], AX.X, ALU.max))
                chain(nc.vector.tensor_tensor(oneh[:, :, :], oneh[:, :, :], wide(lmx), ALU.is_equal))
                dve.wait_ge(lg_exp.sem, lg_exp.at(b, 1))
                chain(nc.vector.tensor_reduce(lsm[:, :], lex[:, :, :], AX.X, ALU.add))
                chain(nc.vector.reciprocal(gate[:, :], lsm[:, :]))
                chain(nc.vector.tensor_tensor(wte[:, :, :], oneh[:, :, :], wide(gate), ALU.mult))
                assert a_dve.here == F_WT
                dve.wait_ge(b2_ps.sem, b2_ps.at(b, 1))
                dve.wait_ge(stored.sem, stored.at(b, 0))
                chain(nc.vector.tensor_tensor(acc[:, :, :], x2[:, :, :], ps[:, 5, :].rearrange("p (t d) -> p t d", t=T), ALU.add))
                assert a_dve.here == F_ACC

            def add_expert(b, e):
                dve.wait_ge(ye_ps.sem, ye_ps.at(b, e + 1))
                dve.wait_ge(ye_acc.sem, ye_acc.at(b, e))
                for t in range(T):
                    last = nc.vector.scalar_tensor_tensor(out=acc[:, t, :], in0=ps[:, 6 + e % 2, t * P:(t + 1) * P],
                                                          scalar=wte[:, t, e:e + 1], in1=acc[:, t, :],
                                                          op0=ALU.mult, op1=ALU.add)
                ye_acc.by(last)

            def expert(b, e):
                dve.wait_ge(ye_ps.sem, ye_ps.at(b, max(e - 1, 0)))
                for f in range(1, FC, 2):
                    dve.wait_ge(h1_ps.sem, h1_ps.at(b, FC * e + f + 1))
                    h1_dve.by(nc.vector.tensor_scalar(h1[:, e % 2, f, :], ps[:, 5, :], b1c[:, e, f:f + 1], 0.0, ALU.add, ALU.max))
                if e:
                    add_expert(b, e - 1)

            walk({"m_norm": m_norm, "m_conv": m_conv, "m_proj": m_proj, "m_soft": m_softplus, "scan": scan, "m_out": m_out,
                  "a_norm": a_norm, "qkv": qkv, "smax": smax, "negm": negm_rows, "exp": exp,
                  "pv": lambda b, g: take_pv(b, 0, g), "o_norm": o_norm, "q2": q2, "cmax": cmax, "cexp": cexp,
                  "cpv": lambda b, g: take_pv(b, 1, g), "f_norm": f_norm, "route": route, "expert": expert, "ye": add_expert})

        @block.tensor
        def _(pe):
            mm = nc.tensor.matmul
            pe.wait_ge(pool_once, POOL_ONCE)
            pe.wait_ge(dve_once, DVE_ONCE)
            pe.wait_ge(loaded, FIRST * 16)

            def tr(to, src, n=P):
                return nc.tensor.transpose(to, src, ident[0:n, 0:n])

            def m_norm(b, _):
                pe.wait_ge(m_dve.sem, m_dve.at(b, 3 * T))
                pe.wait_ge(m_x1.sem, m_x1.at(b, 0))
                for t in range(T):
                    last = tr(ps[:, 2, t * P:(t + 1) * P], mxn[:, t, :])
                m_xnt_ps.by(last)

            def m_in(b, _):
                pe.wait_ge(m_xnt.sem, m_xnt.at(b, 1))
                for c in range(2 * DT):
                    m_xz.by(mm(ps[:, c, :], w_in[:, c * P:(c + 1) * P], mxnT[:, :], start=True, stop=True))

            def m_proj(b, _):
                pe.wait_ge(m_silu.sem, m_silu.at(b, 2))
                pe.wait_ge(m_xin.sem, m_xin.at(b, 2))
                for d in range(DT):
                    last = mm(ps[0:AUG, 0, :], w_xp[:, d, :], xc[:, d, :], start=(d == 0), stop=(d == DT - 1))
                m_xp_ps.by(last)
                for d in range(DT):
                    last = mm(ps[0:AUG, 1, :], w_bc[:, d, :, :].rearrange("p j n -> p (j n)"), xc[:, d, :],
                              start=(d == 0), stop=(d == DT - 1))
                m_xp_ps.by(last)
                pe.wait_ge(m_xdbl.sem, m_xdbl.at(b, 1))
                for d in range(DT):
                    m_dt_ps.by(mm(ps[:, 2 + d, :], w_dt[:, d * P:(d + 1) * P], xdbl[:, :], start=True, stop=True))

            def m_softplus(b, _):
                pe.wait_ge(m_dve.sem, m_dve.at(b, M_BC))
                spread_b(b, 0)

            def spread_b(b, n):
                if n == 0:
                    pe.wait_ge(m_soft.sem, m_soft.at(b, 2))
                    pe.wait_ge(m_dve.sem, m_dve.at(b, M_DT))
                pe.wait_ge(driven.sem, driven.at(b, n))
                b_bc.by(mm(ps[:, 2, :], select[:, n, :], bcs[:, :], start=True, stop=True))

            def sum_states(b, n):
                pe.wait_ge(weighed.sem, weighed.at(b, n + 1))
                for d in range(DT):
                    last = mm(ps[:, d, :], ident[:, :], st[:, n % RING, d, :], start=(n == 0), stop=(n == N - 1))
                summed.by(last)

            def scan(b, n):
                if n == 0:
                    pe.wait_ge(m_dve.sem, m_dve.at(b, M_DT))
                pe.wait_ge(weighed.sem, weighed.at(b, n))
                c_bc.by(mm(ps[:, 3, :], select[:, N + n, :], bcs[:, :], start=True, stop=True))
                if n + 1 < N:
                    spread_b(b, n + 1)
                if n:
                    sum_states(b, n - 1)

            def m_out(b, _):
                sum_states(b, N - 1)
                pe.wait_ge(m_dve.sem, m_dve.at(b, M_YZ))
                for t in range(T):
                    for d in range(DT):
                        last = mm(ps[:, 2, t * P:(t + 1) * P], yz[:, d, t * P:(t + 1) * P], w_out[:, d, :],
                                  start=(d == 0), stop=(d == DT - 1))
                m_out_ps.by(last)

            def a_norm(b, _):
                pe.wait_ge(a_dve.sem, a_dve.at(b, A_XN))
                pe.wait_ge(h1_act.sem, h1_act.at(b, 0))
                for t in range(T):
                    last = tr(ps[:, 4, t * P:(t + 1) * P], axn[:, t, :])
                a_xnt_ps.by(last)
                pe.wait_ge(ctx_in.sem, ctx_in.at(b, 32))
                pe.wait_ge(h1_dve.sem, h1_dve.at(b, 0))
                tr(ps[:, 5, 0:P], ctok[:, 0, :])
                ct_ps.by(tr(ps[:, 5, P:SK], ctok[0:SK - P, 1, :], SK - P))

            def qkv(b, _):
                if b == 0:
                    pe.wait_ge(loaded_rest, REST * 16)
                    pe.wait_ge(turned, 4)
                pe.wait_ge(a_xnt.sem, a_xnt.at(b, 1))
                pe.wait_ge(ye_acc.sem, ye_acc.at(b, 0))
                qk_ps.by(mm(ps[:, 6, :], wq[0][:, :], axnT[:, :], start=True, stop=True))
                qk_ps.by(mm(ps[:, 7, :], wk[0][:, :], axnT[:, :], start=True, stop=True))
                for t in range(T):
                    last = mm(ps[:, 4, t * P:(t + 1) * P], axnT[:, t * P:(t + 1) * P], wv[0][:, :], start=True, stop=True)
                v_ps.by(last)

            def smax(b, g):
                i, h0, per = SELF_MAX[g]
                w = P * (i + 1)
                if g == 0:
                    pe.wait_ge(stacked.sem, stacked.at(b, 128))
                    pe.wait_ge(a_dve.sem, a_dve.at(b, A_V1))
                    pe.wait_ge(ct_sb.sem, ct_sb.at(b, 2))
                elif g == 1:
                    pe.wait_ge(qk_act.sem, qk_act.at(b, 4))
                else:
                    pe.wait_ge(s_max.sem, s_max.at(b, g - 1))
                for n in range(2 * per):
                    h, bank, at = h0 + n, 4 + 2 * (g % 2) + n // per, (n % per) * w
                    mm(ps[:, bank, at:at + w], q_stack[0:AUG, h, i * P:(i + 1) * P], k_stack[0:AUG, h, 0:w],
                       start=True, stop=False)
                    last = mm(ps[:, bank, at + i * P:at + w], identb[:, :], mask_q[:, :], start=False, stop=True)
                s_max_ps.by(last)

            def cmax(b, g):
                i, h0, n = CROSS_MAX[g]
                per = n // 2
                if g == 0:
                    pe.wait_ge(stacked.sem, stacked.at(b, 256))
                    pe.wait_ge(a_dve.sem, a_dve.at(b, A_V2))
                    pe.wait_ge(hT_sb.sem, hT_sb.at(b, 1))
                elif g == 1:
                    pe.wait_ge(qk_act.sem, qk_act.at(b, 10))
                else:
                    pe.wait_ge(s_max.sem, s_max.at(b, len(SELF_MAX) + g - 1))
                for m in range(n):
                    h, bank, at = h0 + m, 4 + 2 * (g % 2) + m // per, (m % per) * SK
                    last = mm(ps[:, bank, at:at + SK], q_stack[0:AUG, h, i * P:(i + 1) * P], k2_stack[0:AUG, h, 0:SK],
                              start=True, stop=True)
                s_max_ps.by(last)

            def negm_rows(b, a):
                pe.wait_ge(a_dve.sem, a_dve.at(b, A_NM[a]))
                for i in range(T):
                    last = mm(ps[0:PARTS * H, 4, i * P:(i + 1) * P], nmp[:, i, :, :].rearrange("p j h -> p (j h)"), identb[:, :],
                              start=True, stop=True)
                nm_ps.by(last)

            def times_v(b, g):
                pe.wait_ge(probs.sem, probs.at(b, 3 * GH * (g + 1)))
                pe.wait_ge(pv_sb.sem, pv_sb.at(b, g))
                for j in range(T):
                    for c in range(GH):
                        last = mm(ps[32 * c:32 * c + 32, 7, j * P:L], v1a[:, j, GH * g + c, :],
                                  pth[:, (GH * g + c) % PT_HEADS, PT_AT[j]:PT_AT[j] + L - j * P], start=(j == 0), stop=(j == T - 1))
                pv_ps.by(last)

            def exp(b, h):
                if h == 0:
                    pe.wait_ge(nm_in.sem, nm_in.at(b, 48))
                    pe.wait_ge(nm_sb.sem, nm_sb.at(b, 1))
                for n, (base, _, tiles) in enumerate(PT_UNITS):
                    r = 3 * h + n
                    if h:
                        pe.wait_ge(probs.sem, probs.at(b, r - 2))
                    for j in tiles:
                        at, w = PT_AT[j] - base, L - j * P
                        mm(ps[:, 4 + r % 3, at:at + w], k_stack[0:KAUG, h, j * P:(j + 1) * P], q_stack[0:KAUG, h, j * P:L],
                           start=True, stop=False)
                        last = mm(ps[:, 4 + r % 3, at:at + P], identb[:, :], mask_k[:, :], start=False, stop=True)
                    sc_ps.by(last)
                if h % GH == 1 and h > GH:
                    times_v(b, h // GH - 1)

            def times_v2(b, g):
                n = H // GH + g
                pe.wait_ge(probs.sem, probs.at(b, 3 * H + (GH + 1) * (g + 1)))
                pe.wait_ge(pv_sb.sem, pv_sb.at(b, n))
                for c in range(GH):
                    mm(ps[32 * c:32 * c + 32, 7, :], v2a[:, GH * g + c, :], cross(g, c), start=True, stop=False)
                for c in range(GH):
                    last = mm(ps[32 * c:32 * c + 32, 7, :], v2b[:, GH * g + c, :], cross(g, GH), start=False, stop=True)
                pv_ps.by(last)

            def cexp(b, g):
                if g == 0:
                    pe.wait_ge(nm_in.sem, nm_in.at(b, 96))
                    pe.wait_ge(nm_sb.sem, nm_sb.at(b, 2))
                for n in range(GH + 1):
                    m = (GH + 1) * g + n
                    r = 3 * H + m
                    if m >= 3:
                        pe.wait_ge(probs.sem, probs.at(b, r - 2))
                    if n < GH:
                        last = mm(ps[:, 4 + r % 3, :], k2_stack[0:KAUG, GH * g + n, 0:P], q_stack[0:KAUG, GH * g + n, :],
                                  start=True, stop=True)
                    else:
                        for c in range(GH):
                            last = mm(ps[32 * c:32 * c + 32, 4 + r % 3, :], k2_stack[0:KAUG, GH * g + c, P:SKP],
                                      q_stack[0:KAUG, GH * g + c, :], start=True, stop=True)
                    sc_ps.by(last)
                if g:
                    times_v2(b, g - 1)

            def o_norm(b, a):
                pe.wait_ge(pv_sb.sem, pv_sb.at(b, (a + 1) * H // GH))
                pe.wait_ge(probs.sem, probs.at(b, (3 * H, 3 * H + (GH + 1) * H // GH)[a]))
                for i in range(T):
                    for g in range(GH):
                        last = mm(ps[:, 4 + i, g * P:(g + 1) * P], ot[:, g, i * P:(i + 1) * P], ident[:, :], start=True, stop=True)
                    ot_ps.by(last)
                pe.wait_ge(o_tok.sem, o_tok.at(b, T * (a + 1)))
                for i in range(T):
                    last = tr(ps[:, 4, i * P:(i + 1) * P], otok[:, i, :])
                oT_ps.by(last)
                pe.wait_ge(oT_sb.sem, oT_sb.at(b, a + 1))
                if a:
                    for i in range(T):
                        last = mm(ps[:, 5, i * P:(i + 1) * P], oT[:, i * P:(i + 1) * P], wo[1][:, :], start=True, stop=True)
                    o2_ps.by(last)

            def q2(b, _):
                hT_ps.by(mm(ps[:, 5, :], wo[0][:, :], oT[:, :], start=True, stop=True))
                wk2 = wk[1][:, :]
                pe.wait_ge(ct_sb.sem, ct_sb.at(b, 2))
                mm(ps[:, 7, 0:P], wk2, ctxT[:, :], start=True, stop=True)
                last = mm(ps[:, 7, P:SK], wk2, ctx4[:, 0, 0:SK - P], start=True, stop=True)
                mm(ps[:, 4, 0:P], ctxT[:, :], wv[1][:, :], start=True, stop=True)
                v_ps.by(mm(ps[:, 4, P:2 * P], ctx4[:, :, :].rearrange("d c k -> d (c k)"), wv[1][:, :], start=True, stop=True))
                pe.wait_ge(hT_sb.sem, hT_sb.at(b, 1))
                qk_ps.by(mm(ps[:, 6, :], wq[1][:, :], hT[:, :], start=True, stop=True), 2)

            def f_norm(b, _):
                pe.wait_ge(a_dve.sem, a_dve.at(b, F_XN))
                for t in range(T):
                    last = tr(ps[:, 4, t * P:(t + 1) * P], axn[:, t, :])
                f_xnt_ps.by(last)

            def route(b, _):
                pe.wait_ge(f_xnt.sem, f_xnt.at(b, 1))
                for t in range(T):
                    last = mm(ps[:, 6, t * E:(t + 1) * E], axnT[:, t * P:(t + 1) * P], wr[:, :], start=True, stop=True)
                lg_ps.by(last)
                pe.wait_ge(a_dve.sem, a_dve.at(b, F_WT))
                for t in range(T):
                    last = mm(ps[0:E, 7, t * P:(t + 1) * P], wte[:, t, :], ident[:, :], start=True, stop=True)
                wt_ps.by(last)
                pe.wait_ge(wt_sb.sem, wt_sb.at(b, 1))
                for t in range(T):
                    last = mm(ps[:, 5, t * P:(t + 1) * P], wteT[:, t * P:(t + 1) * P], b2r[:, :], start=True, stop=True)
                b2_ps.by(last)

            def down(b, e):
                pe.wait_ge(h1_act.sem, h1_act.at(b, 2 * (e + 1)))
                pe.wait_ge(h1_dve.sem, h1_dve.at(b, 2 * (e + 1)))
                pe.wait_ge(ye_acc.sem, ye_acc.at(b, max(e - 1, 0)))
                for t in range(T):
                    for f in range(FC):
                        last = mm(ps[:, 6 + e % 2, t * P:(t + 1) * P], h1[:, e % 2, f, t * P:(t + 1) * P], w2[:, e, f, :],
                                  start=(f == 0), stop=(f == FC - 1))
                ye_ps.by(last)

            def expert(b, e):
                for f in range(FC):
                    if e == 0 and f < 2:
                        pe.wait_ge(a_dve.sem, a_dve.at(b, F_ACC))
                    else:
                        done = h1_act if f % 2 == 0 else h1_dve
                        pe.wait_ge(done.sem, done.at(b, 2 * e + f // 2))
                    h1_ps.by(mm(ps[:, 4 + f % 2, :], w1[:, e, f * P:(f + 1) * P], axnT[:, :], start=True, stop=True))
                if e:
                    down(b, e - 1)

            walk({"m_norm": m_norm, "m_in": m_in, "m_proj": m_proj, "m_soft": m_softplus, "scan": scan, "m_out": m_out,
                  "a_norm": a_norm, "qkv": qkv, "smax": smax, "negm": negm_rows, "exp": exp, "pv": times_v,
                  "o_norm": o_norm, "q2": q2, "cmax": cmax, "cexp": cexp, "cpv": times_v2,
                  "f_norm": f_norm, "route": route, "expert": expert, "ye": down})

        for s in signals:
            assert s.seen == B * s.per_batch, (s.name, s.seen, B * s.per_batch)


_INS = ["x", "ctx_1024", "L0_attn_W_in", "L0_attn_conv_w", "L0_attn_conv_b", "L0_attn_W_xproj", "L0_attn_W_dt",
        "L0_attn_b_dt", "L0_attn_A_log", "L0_attn_Dp", "L0_attn_W_out",
        "L0_xattn_Wq1", "L0_xattn_bq1", "L0_xattn_Wk1", "L0_xattn_bk1", "L0_xattn_Wv1", "L0_xattn_bv1",
        "L0_xattn_Wo1", "L0_xattn_bo1", "L0_xattn_Wq2", "L0_xattn_bq2", "L0_xattn_Wk2", "L0_xattn_bk2",
        "L0_xattn_Wv2", "L0_xattn_bv2", "L0_xattn_Wo2", "L0_xattn_bo2",
        "L0_ffn_Wr", "L0_ffn_br", "L0_ffn_W1", "L0_ffn_b1", "L0_ffn_W2", "L0_ffn_b2"]


def kernel(**inputs):
    import numpy as _np
    import concourse.bacc as _bacc
    from concourse import mybir as _mybir
    from concourse.bass_utils import run_bass_kernel_spmd as _run

    nc = _bacc.Bacc("TRN2", target_bir_lowering=False, num_devices=1)
    arrays, args = {}, []
    for name in _INS:
        a = _np.ascontiguousarray(inputs[name])
        arrays[f"in_{name}"] = a
        args.append(nc.dram_tensor(f"in_{name}", a.shape, _mybir.dt.from_np(a.dtype), kind="ExternalInput").ap())
    for name in ("q_scratch", "k_scratch"):
        args.append(nc.dram_tensor(name, (PARTS, P, L), _mybir.dt.bfloat16, kind="Internal").ap())
    args.append(nc.dram_tensor("out_x", (B, L, D), _mybir.dt.float32, kind="ExternalOutput").ap())
    decoder_kernel(nc, *args)
    return _run(nc, [arrays], core_ids=[0]).results[0]["out_x"]
```

```python
from contextlib import ExitStack

import concourse.bass as bass
from concourse import mybir

FP32 = mybir.dt.float32
BF16 = mybir.dt.bfloat16
ALU = mybir.AluOpType
ACT = mybir.ActivationFunctionType
AX = mybir.AxisListType

P = 128
B, L, D = 4, 512, 128
T = L // P
DI, DT = 256, 2
RING = 3
N = 16
RANK = 64
CONV = 4
H, HD = 16, 8
SK, SKP = 154, 160
TAIL = SKP - P
PARTS = 3
PROD = PARTS * PARTS * HD
AUG = 96
KAUG = AUG + PARTS
GH = 4
E, FF = 8, 512
FC = FF // P
FIRST, REST = 9, 51
POOL_EARLY, POOL_ONCE, DVE_EARLY, DVE_ONCE = 6, 33, 4, 8
M_STAT, M_XN, M_CONV, M_BC, M_DT, M_YZ = 9, 13, 21, 26, 29, 33
A_STAT, A_XN, A_V1, A_NM, A_V2 = 9, 13, 17, (21, 34), 30
A_OUT = 39
F_STAT, F_XN, F_LOGITS, F_WT, F_ACC = 9, 13, 16, 23, 24
QK_BANK = (6, 5)
SCALE = float(HD) ** -0.5
NEG = -3.0e38
STACKED = 16 * 2 * PARTS * PARTS
EPS = 1e-5
SNAP = 16
H1_RING = FC + 2
PT_HEADS = 6
CAUSAL = sum((L - P * j) for j in range(T))
PT_AT = [0, 512, 1024, 896]
PT_UNITS = [(0, 512, [0]), (512, 512, [1, 3]), (1024, 256, [2])]


class Batch:

    def __init__(self, turn, lead):
        self.turn, self.lead = turn, lead
        self.index = turn + lead
        self.first = isinstance(turn, int) and turn + lead == 0


class Signal:

    def __init__(self, nc, ctx, name, per_batch):
        self.name, self.per_batch = name, per_batch
        self.sem = ctx.enter_context(nc.semaphore(name))
        self.seen = 0
        self.here = 0

    def start(self):
        self.here = 0

    def at(self, b, k):
        return b.turn * self.per_batch + (b.lead * self.per_batch + k)

    def by(self, instruction, amount=1):
        instruction.then_inc(self.sem, amount)
        self.seen += amount
        self.here += amount

    def settle(self, engine, b, but=0):
        engine.wait_ge(self.sem, self.at(b, self.here - but))


def merge(main, *others):
    lead, chain = main
    placed = [(i + 0.5, lead, name, k) for i, (name, k, *_) in enumerate(chain)]
    for n, (lead, other) in enumerate(others):
        rooms = [step[2 + n] for step in chain]
        total, at = sum(w for *_, w in other), 0.0
        i, before = 0, 0.0
        for name, k, w in other:
            wanted = (at + w / 2) / total * sum(rooms)
            while before + rooms[i] < wanted:
                before += rooms[i]
                i += 1
            placed.append((i + (wanted - before) / rooms[i], lead, name, k))
            at += w
    return [step[1:] for step in sorted(placed, key=lambda step: step[0])]


def decoder_kernel(nc, x, ctx_tokens, W_in, conv_w, conv_b, W_xproj, W_dt, b_dt, A_log, Dp, W_out,
                   Wq1, bq1, Wk1, bk1, Wv1, bv1, Wo1, bo1, Wq2, bq2, Wk2, bk2, Wv2, bv2, Wo2, bo2,
                   Wr, br, W1, b1, W2, b2, out):
    ctx = ExitStack()
    with ctx:
        def sb(name, shape, dt=FP32):
            return ctx.enter_context(nc.sbuf_tensor(name, shape, dt))

        signals = []

        def sig(name, per_batch):
            signals.append(Signal(nc, ctx, name, per_batch))
            return signals[-1]

        def once(name):
            return ctx.enter_context(nc.semaphore(name))

        w_in = sb("w_in", [P, 2 * DI])
        w_xp = sb("w_xp", [P, DT, AUG])
        w_bc = sb("w_bc", [P, DT, PARTS, 2 * N])
        w_dt = sb("w_dt", [AUG, DI])
        w_out = sb("w_out", [P, DT, D])
        cw = sb("cw", [P, DT, CONV])
        cb = sb("cb", [P, DT])
        bdt = sb("bdt", [P, DT])
        a_neg = sb("a_neg", [P, DT, N])
        a_log = sb("a_log", [P, DT, N])
        dp = sb("dp", [P, DT])
        wq, wk, wv, wo = ([sb(f"w{c}{i}", [P, D]) for i in (1, 2)] for c in "qkvo")
        bq, bk, bocol = ([sb(f"b{c}{i}", [P, 1]) for i in (1, 2)] for c in ("q", "k", "oc"))
        bvrow = [sb(f"bv{i}r", [P, D]) for i in (1, 2)]
        bo2row = sb("bo2r", [P, D])
        wr = sb("wr", [P, E])
        brrow = sb("brr", [P, E])
        w1 = sb("w1", [P, E, FF])
        w2 = sb("w2", [P, E, FC, D])
        b1c = sb("b1c", [P, E, FC])
        b2r = sb("b2r", [E, D])

        ident = sb("ident", [P, P])
        identb = sb("identb", [P, P], BF16)
        mask_q = sb("mask_q", [P, P], BF16)
        mask_k = sb("mask_k", [P, P], BF16)
        select = sb("select", [AUG, 2 * N], BF16)
        eps = sb("eps", [P, 1])
        prefer = sb("prefer", [P, E])

        x_tok = sb("x_tok", [P, T, D])
        mst = sb("mst", [P, T, 6])
        mmv = sb("mmv", [P, T, 2])
        mrs = sb("mrs", [P, T])
        xin = sb("xin", [P, DT, CONV - 1 + L])
        conv = sb("conv", [P, DT, L])
        sz = sb("sz", [P, DT, L])
        mxn = sz[:, 0, :].rearrange("p (t d) -> p t d", t=T)
        xc = sb("xc", [P, DT, L])
        bcs = sb("bcs", [AUG, L], BF16)
        bcm = sb("bcm", [AUG, L], BF16)
        spa = conv
        dts = sb("dts", [P, DT, L])
        u = sb("u", [P, DT, L])
        mxnT = u[:, 0, :]
        dA = sb("dA", [P, 2, DT, L])
        st = sb("st", [P, RING, DT, L])
        xdbl = st[0:AUG, RING - 1, 0, :]
        bcr = st[0:AUG, RING - 1, 1, :]
        ysum = yz = conv

        x1 = sb("x1", [P, T, D])
        ast = sb("ast", [P, T, 6])
        amv = sb("amv", [P, T, 2])
        ars = sb("ars", [P, T])
        axn = sb("axn", [P, T, D])
        axnT = sb("axnT", [P, L])
        ctok = sb("ctok", [P, 2, D])
        ctxT = sb("ctxT", [P, P])
        ctx4 = sb("ctx4", [P, GH, TAIL])
        ot = sb("ot", [P, GH, L])
        qp = ot[:, 0:3, :].bitcast(BF16).rearrange("p a (b t) -> p (a b) t", t=L).rearrange("p (i j) t -> p i j t", i=2)
        q_stack = sb("q_stack", [P, H, L], BF16)
        k_stack = sb("k_stack", [P, H, L], BF16)
        k2_stack = sb("k2_stack", [P, H, SKP], BF16)
        v1a = sb("v1a", [P, T, H, 32])
        v2a = sb("v2a", [P, H, 32])
        v2b = sb("v2b", [P, H, 32])
        negm = sb("negm", [P, T, H])
        nmr = sb("nmr", [P, T, H])
        nmp = sb("nmp", [P, T, PARTS, H], BF16)
        nmT = sb("nmT", [PARTS * H, L], BF16)
        pt = sb("pt", [P, PT_HEADS * CAUSAL])
        pth = pt[:, :].rearrange("p (s c) -> p s c", s=PT_HEADS)
        qf = pt[:, 0:2 * L].rearrange("p (i t) -> p i t", i=2)
        qr = pt[:, 2 * L:4 * L].rearrange("p (i t) -> p i t", i=2)
        orc = sb("orc", [P, T, H])
        otok = axn
        oT = axn[:, :, :].rearrange("p t d -> p (t d)")
        hT = axnT
        lg = sb("lg", [P, T, E])
        lmx = sb("lmx", [P, T])
        lex = sb("lex", [P, T, E])
        lsm = sb("lsm", [P, T])
        gate = sb("gate", [P, T])
        oneh = sb("oneh", [P, T, E])
        wte = sb("wte", [P, T, E])
        acc = sb("acc", [P, T, D])
        fst = sb("fst", [P, T, 6])
        fmv = sb("fmv", [P, T, 2])
        frs = sb("frs", [P, T])
        h1 = sb("h1", [P, H1_RING, L])
        fxn = h1[:, H1_RING - 1, :].rearrange("p (t d) -> p t d", t=T)
        fxnT = sb("fxnT", [P, L])
        wteT = h1[0:E, H1_RING - 1, :]

        def cross(g, n):
            at = ((GH + 1) * (g % 2) + n) * L
            return pt[:, at:at + L]

        ps = ctx.enter_context(nc.psum_tensor("ps", [P, 8, 512], FP32))

        loaded = once("loaded")
        loaded_rest = once("loaded_rest")
        pool_once = once("pool_once")
        dve_once = once("dve_once")
        act_once = once("act_once")
        turned = once("turned")

        SELF_MAX = []
        for i in range(T):
            per_bank = L // (P * (i + 1))
            SELF_MAX += [(i, h0, per_bank) for h0 in range(0, H, per_bank)]
        CROSS_MAX = [(i, h0, min(3, H - h0)) for i in range(T) for h0 in range(0, H, 3)]

        x_in = sig("x_in", 16)
        m_dve = sig("m_dve", M_YZ)
        m_rstd = sig("m_rstd", 2)
        m_xnt_ps = sig("m_xnt_ps", 1)
        m_xnt = sig("m_xnt", 1)
        m_xz = sig("m_xz", 4)
        m_xin = sig("m_xin", 2)
        m_silu = sig("m_silu", 2)
        m_xp_ps = sig("m_xp_ps", 2)
        m_xdbl = sig("m_xdbl", 1)
        m_dt_ps = sig("m_dt_ps", 2)
        m_soft = sig("m_soft", 4)
        b_bc = sig("b_bc", N)
        c_bc = sig("c_bc", N)
        decay = sig("decay", N)
        driven = sig("driven", N)
        scanned = sig("scanned", 2 * N)
        weighed = sig("weighed", N)
        summed = sig("summed", N)
        m_out_ps = sig("m_out_ps", 1)
        m_x1 = sig("m_x1", 1)

        ctx_in = sig("ctx_in", 32)
        a_dve = sig("a_dve", A_OUT)
        f_dve = sig("f_dve", F_ACC)
        a_x2 = sig("a_x2", 1)
        a_rstd = sig("a_rstd", 2)
        a_xnt_ps = sig("a_xnt_ps", 1)
        a_xnt = sig("a_xnt", 1)
        qk_ps = sig("qk_ps", 4)
        v_ps = sig("v_ps", 2)
        qk_act = sig("qk_act", 12)
        qk_parts = sig("qk_parts", 8)
        stacked = sig("stacked", 2 * STACKED)
        s_max_ps = sig("s_max_ps", len(SELF_MAX) + len(CROSS_MAX))
        s_max = sig("s_max", len(SELF_MAX) + len(CROSS_MAX))
        nm_ps = sig("nm_ps", 2)
        nm_sb = sig("nm_sb", 2)
        nm_in = sig("nm_in", 32)
        sc_ps = sig("sc_ps", 3 * H + 5 * H // GH)
        probs = sig("probs", 3 * H + 5 * H // GH)
        pv_ps = sig("pv_ps", 2 * H // GH)
        pv_sb = sig("pv_sb", 2 * H // GH)
        ot_ps = sig("ot_ps", 2 * T)
        o_tok = sig("o_tok", 2 * T)
        oT_ps = sig("oT_ps", 2)
        oT_sb = sig("oT_sb", 2)
        hT_ps = sig("hT_ps", 1)
        hT_sb = sig("hT_sb", 1)
        ct_ps = sig("ct_ps", 1)
        ct_sb = sig("ct_sb", 2)
        o2_ps = sig("o2_ps", 1)
        f_rstd = sig("f_rstd", 2)
        f_xnt_ps = sig("f_xnt_ps", 1)
        f_xnt = sig("f_xnt", 1)
        lg_ps = sig("lg_ps", 1)
        lg_exp = sig("lg_exp", 1)
        wt_ps = sig("wt_ps", 1)
        wt_sb = sig("wt_sb", 1)
        b2_ps = sig("b2_ps", 1)
        h1_ps = sig("h1_ps", E * FC)
        h1_act = sig("h1_act", E * FC)
        ye_ps = sig("ye_ps", E)
        ye_acc = sig("ye_acc", E)
        acc_free = sig("acc_free", 16)

        MAMBA = [("m_norm", 0, 5.293), ("m_norm2", 0, 4), ("m_in", 0, 5), ("m_conv", 0, 7), ("m_proj", 0, 3.389), ("m_soft", 0, 8)]
        for n in range(N):
            MAMBA += [("scan", n, 0.351)] + [("drive", n + 1, 2)] * (n + 1 < N) + [("weigh", n, 2)]
        MAMBA += [("m_out", 0, 4), ("m_out2", 0, 4)]
        ATTEND = [("a_norm", 0, 10.36, 2.454), ("a_norm2", 0, 2, 2), ("qkv", 0, 5, 5), ("stack", 0, 15, 16)]
        ATTEND += [("smax", g, 0.15, 0.023) for g in range(len(SELF_MAX))] + [("negm", 0, 8, 9.373)]
        ATTEND += [("exp", r, 0.1, 0.7) for r in range(3 * H)] + [("pv", H // GH - 1, 2.218, 3.88)]
        ATTEND += [("o_norm", 0, 3.353, 3), ("q2", 0, 1.012, 5.346), ("stack", 1, 15, 16)]
        ATTEND += [("cmax", g, 0.203, 0.293) for g in range(len(CROSS_MAX))] + [("negm", 1, 8, 7.325)]
        ATTEND += [("cexp", r, 0.3, 0.7) for r in range((GH + 1) * H // GH)] + [("cpv", H // GH - 1, 2.023, 1.29)]
        ATTEND += [("o_norm", 1, 4, 3.074), ("o_out", 0, 1.001, 2)]
        FEED = [("f_norm", 0, 1), ("f_norm2", 0, 3), ("f_logits", 0, 3), ("up", 0, 2.02), ("f_logits2", 0, 3), ("up", 1, 2.02),
                ("f_route", 0, 6.085), ("up", 2, 2.02), ("f_bias", 0, 3), ("up", 3, 2.02)]
        for e in range(1, E + 1):
            for f in range(FC):
                FEED += [("up", FC * e + f, 1.5)] * (e < E)
                if f < 2:
                    FEED += [("down", T * (e - 1) + 2 * f, 1.5), ("down", T * (e - 1) + 2 * f + 1, 1.5)]
        FEED += [("store", 0, 2.42)]
        STEPS = merge((1, ATTEND), (0, FEED), (2, MAMBA))

        def walk(engine, steps, ahead=None):
            def turn(t, leads, copy=None):
                mine = [step for step in STEPS if step[0] in leads and step[1] in steps]
                for n, (lead, name, k) in enumerate(mine):
                    if n % SNAP == 0 and not isinstance(t, int) and not ahead:
                        engine.reg_mov(copy, t)
                        t = engine.snap(copy)
                    steps[name](Batch(t, lead), k)

            turn(-2, (2,))
            turn(-1, (2, 1))
            with engine.register("turn") as copy, engine.Fori(0, B - 2) as t:
                if ahead:
                    ahead(t)
                turn(t, (2, 1, 0), copy)
            turn(B - 2, (1, 0))
            turn(B - 1, (0,))

        ctx.enter_context(nc.allow_non_contiguous_dma(reason="biases go to partitions once"))
        block = ctx.enter_context(nc.Block())

        @block.sync
        def _(sp):
            first = [
                (w_in[:, :], W_in), (w_xp[:, :, :], W_xproj.rearrange("(d p) e -> p d e", p=P)),
                (w_dt[0:RANK, :], W_dt), (w_out[:, :, :], W_out.rearrange("(d p) e -> p d e", p=P)),
                (cw[:, :, :], conv_w.rearrange("(d p) k -> p d k", p=P)),
                (cb[:, :], conv_b.rearrange("(d p) -> p d", p=P)),
                (bdt[:, :], b_dt.rearrange("(d p) -> p d", p=P)),
                (a_log[:, :, :], A_log.rearrange("(d p) n -> p d n", p=P)),
                (dp[:, :], Dp.rearrange("(d p) -> p d", p=P)),
            ]
            rest = []
            for i, (q, k, v, o) in enumerate([(Wq1, Wk1, Wv1, Wo1), (Wq2, Wk2, Wv2, Wo2)]):
                for to, w in ((acc[:, 2 * i, :], q), (acc[:, 2 * i + 1, :], k), (wv[i][:, :], v)):
                    rest.append((to.rearrange("d (h e) -> d h e", h=H), w.rearrange("h d e -> d h e")))
                rest.append((wo[i][:, :], o))
            for i, (q, k, v, o) in enumerate([(bq1, bk1, bv1, bo1), (bq2, bk2, bv2, bo2)]):
                for e in range(HD):
                    rest.append((bq[i][e * H:(e + 1) * H, :], q[:, e:e + 1]))
                    rest.append((bk[i][e * H:(e + 1) * H, :], k[:, e:e + 1]))
                rest.append((bvrow[i][:, :], v.rearrange("h e -> (h e)").partition_broadcast(P)))
                rest.append((bocol[i][:, :], o.rearrange("(e o) -> e o", o=1)))
            rest += [
                (bo2row[:, :], bo2.partition_broadcast(P)), (wr[:, :], Wr), (brrow[:, :], br.partition_broadcast(P)),
                (w1[:, :, :], W1.rearrange("e h f -> h e f")),
                (w2[:, :, :, :], W2.rearrange("e (c p) h -> p e c h", p=P)),
                (b1c[:, :, :], b1.rearrange("e (c p) -> p e c", p=P)), (b2r[:, :], b2),
            ]
            assert len(first) == FIRST and len(rest) == REST

            def m_norm(b, _):
                if not b.first:
                    sp.wait_ge(a_dve.sem, a_dve.at(b, T + 1 - a_dve.per_batch))
                x_in.by(sp.dma_start(x_tok[:, :, :], x[b.index].rearrange("(t p) d -> p t d", p=P)), 16)
                if b.first:
                    for to, src in first:
                        sp.dma_start(to, src).then_inc(loaded, 16)
                    for to, src in rest:
                        sp.dma_start(to, src).then_inc(loaded_rest, 16)

            def a_norm(b, _):
                sp.wait_ge(ct_ps.sem, ct_ps.at(b, 0))
                ctx_in.by(sp.dma_start(ctok[:, 0, :], ctx_tokens[b.index, 0:P, :]), 16)
                ctx_in.by(sp.dma_start(ctok[0:SK - P, 1, :], ctx_tokens[b.index, P:SK, :]), 16)

            def stack(b, a):
                width, ks = ((L, k_stack), (SK, k2_stack))[a]
                if b.first and a == 0:
                    sp.wait_ge(pool_once, POOL_ONCE)
                sp.wait_ge(sc_ps.sem, sc_ps.at(b, 3 * H * a))
                for j in range(PARTS):
                    if j < 2:
                        sp.wait_ge(qk_act.sem, qk_act.at(b, 6 * a + (2, 5)[j]))
                    else:
                        sp.wait_ge(qk_parts.sem, qk_parts.at(b, 4 * a + 3))
                    for rep in range(PARTS):
                        at = (PARTS * rep + j) * HD
                        stacked.by(sp.dma_start(q_stack[at:at + HD, :, :], qp[:, 0, j, :]), 16)
                    if j < 2:
                        sp.wait_ge(qk_act.sem, qk_act.at(b, 6 * a + (4, 6)[j]))
                    else:
                        sp.wait_ge(qk_parts.sem, qk_parts.at(b, 4 * a + 4))
                    for rep in range(PARTS):
                        at = (PARTS * rep + (j - rep) % PARTS) * HD
                        stacked.by(sp.dma_start(ks[at:at + HD, :, 0:width], qp[:, 1, j, 0:width]), 16)

            def negm_rows(b, a):
                sp.wait_ge(nm_sb.sem, nm_sb.at(b, a + 1))
                nm_in.by(sp.dma_start(q_stack[AUG:KAUG, :, :], nmT[:, :]), 16)

            def store(b, _):
                sp.wait_ge(ye_acc.sem, ye_acc.at(b, E))
                acc_free.by(sp.dma_start(out[b.index].rearrange("(t p) d -> p t d", p=P), acc[:, :, :]), 16)

            def ahead(t):
                m, a, f = Batch(t, 2), Batch(t, 1), Batch(t, 0)
                moved = (x[m.index], out[f.index], ctx_tokens[a.index, 0:P, :], ctx_tokens[a.index, P:SK, :])
                values = [4 * array.offset for array in moved]
                values += [a_dve.at(m, T + 1 - a_dve.per_batch), ct_ps.at(a, 0), ye_acc.at(f, E)]
                for i in range(2):
                    values += [qk_parts.at(a, 4 * i + n) for n in (3, 4)] + [qk_act.at(a, 6 * i + n) for n in (2, 4, 5, 6)]
                    values += [sc_ps.at(a, 3 * H * i), nm_sb.at(a, i + 1)]
                for v in values:
                    sp.lower_val(v)

            walk(sp, {"m_norm": m_norm, "a_norm": a_norm, "stack": stack, "negm": negm_rows, "store": store}, ahead)
            sp.wait_ge(acc_free.sem, acc_free.at(Batch(B, 0), 16))

        @block.gpsimd
        def _(pool):
            pool.memset(ident[:, :], 0.0).then_inc(pool_once, 1)
            pool.memset(select[:, :], 0.0).then_inc(pool_once, 1)
            pool.wait_ge(pool_once, 2)
            pool.affine_select(out=ident[:, :], in_=ident[:, :], compare_op=ALU.not_equal, fill=1.0,
                               base=0, pattern=[[-1, P]], channel_multiplier=1).then_inc(pool_once, 1)
            for j in range(PARTS):
                pool.affine_select(out=select[:, :], in_=select[:, :], compare_op=ALU.not_equal, fill=1.0,
                                   base=-2 * N * j, pattern=[[-1, 2 * N]], channel_multiplier=1).then_inc(pool_once, 1)
                pool.wait_ge(pool_once, 4 + j)
            pool.memset(mask_q[:, :], 0.0).then_inc(pool_once, 1)
            pool.memset(mask_k[:, :], 0.0).then_inc(pool_once, 1)
            pool.wait_ge(pool_once, POOL_EARLY + 2)
            pool.affine_select(out=mask_q[:, :], in_=mask_q[:, :], compare_op=ALU.is_ge, fill=NEG,
                               base=0, pattern=[[-1, P]], channel_multiplier=1).then_inc(pool_once, 1)
            pool.affine_select(out=mask_k[:, :], in_=mask_k[:, :], compare_op=ALU.is_ge, fill=NEG,
                               base=0, pattern=[[1, P]], channel_multiplier=-1).then_inc(pool_once, 1)
            for e in range(E):
                pool.memset(prefer[:, e:e + 1], float(E - e)).then_inc(pool_once, 1)
            pool.memset(v1a[:, :, :, :], 0.0).then_inc(pool_once, 1)
            for view in (v2a, v2b, q_stack, k_stack, k2_stack, ctx4):
                pool.memset(view[:, :, :], 0.0).then_inc(pool_once, 1)
            pool.wait_ge(pool_once, 25)
            ones = [v1a[:, :, :, HD:HD + 1], v2a[:, :, HD:HD + 1]]
            ones += [v2b[32 * c:32 * c + SK - P, :, :].rearrange("p (g c) x -> p g c x", c=GH)[:, :, c, HD:HD + 1] for c in range(GH)]
            ones += [k_stack[AUG:P, :, :], k2_stack[AUG:P, :, 0:SK]]
            for n, view in enumerate(ones):
                pool.memset(view, 1.0).then_inc(pool_once, 1)
                pool.wait_ge(pool_once, 26 + n)

            pool.wait_ge(loaded_rest, REST * 16)
            for i, to in enumerate((wq[0], wk[0], wq[1], wk[1])):
                if i == 3:
                    pool.wait_ge(turned, 3)
                copy = pool.tensor_copy(to[:, :].rearrange("d (e h) -> d h e", h=H),
                                        acc[:, i, :].rearrange("d (h e) -> d h e", h=H))
                copy.then_inc(*((turned, 1) if i < 3 else (acc_free.sem, 16)))

            def split(b, a):
                width = (L, SK)[a]
                for i, w in ((0, L), (1, width)):
                    pool.wait_ge(qk_act.sem, qk_act.at(b, 6 * a + 2 * i + 2))
                    pool.wait_ge(qk_parts.sem, qk_parts.at(b, 4 * a))
                    qk_parts.by(pool.tensor_tensor(qr[:, i, 0:w], qf[:, i, 0:w], qp[:, i, 0, 0:w], ALU.subtract))
                for i, w in ((0, L), (1, width)):
                    pool.wait_ge(qk_act.sem, qk_act.at(b, 6 * a + 5 + i))
                    qk_parts.by(pool.tensor_tensor(qp[:, i, 2, 0:w], qr[:, i, 0:w], qp[:, i, 1, 0:w], ALU.subtract))

            def add_state(b, n):
                if n == 0:
                    summed.start()
                else:
                    pool.wait_ge(weighed.sem, weighed.at(b, n + 1))
                    summed.settle(pool, b)
                    summed.by(pool.tensor_tensor(ysum[:, :, :], st[:, 0, :, :] if n == 1 else ysum[:, :, :],
                                                 st[:, n % RING, :, :], ALU.add), 2 if n == 1 else 1)

            walk(pool, {"weigh": add_state, "qkv": lambda b, _: split(b, 0), "q2": lambda b, _: split(b, 1)})

        @block.scalar
        def _(act):
            nc.scalar.preload_act_table_set("natural_log_exp_and_others")
            act.wait_ge(dve_once, DVE_EARLY)

            def rstd(b, sig, mv, rs, have, at):
                act.wait_ge(have.sem, have.at(b, at))
                sig.by(nc.scalar.activation(rs[:, :], mv[:, :, 1], ACT.Ln, bias=eps[:, 0:1]))
                act.wait_ge(sig.sem, sig.at(b, 1))
                sig.by(nc.scalar.activation(rs[:, :], rs[:, :], ACT.Exp, scale=-0.5))

            def m_norm(b, _):
                rstd(b, m_rstd, mmv, mrs, m_dve, M_STAT)
                if b.first:
                    act.wait_ge(loaded, FIRST * 16)
                    nc.scalar.activation(a_neg[:, :, :], a_log[:, :, :], ACT.Exp).then_inc(act_once, 1)

            def m_in(b, _):
                act.wait_ge(m_xnt_ps.sem, m_xnt_ps.at(b, 1))
                m_xnt.by(nc.scalar.copy(mxnT[:, :], ps[:, 2, :]))
                for d in range(DT):
                    act.wait_ge(m_xz.sem, m_xz.at(b, d + 1))
                    m_xin.by(nc.scalar.copy(xin[:, d, CONV - 1:], ps[:, 2 + d, :]))

            def m_conv(b, _):
                act.wait_ge(m_xz.sem, m_xz.at(b, 4))
                act.wait_ge(m_dve.sem, m_dve.at(b, 0))
                m_silu.by(nc.scalar.activation(sz[:, :, :], ps[:, 2:4, :], ACT.Silu))
                act.wait_ge(m_dve.sem, m_dve.at(b, M_CONV))
                m_silu.by(nc.scalar.activation(xc[:, :, :], conv[:, :, :], ACT.Silu))
                nc.scalar.preload_act_table_set("natural_log_exp_and_others")

            def m_proj(b, _):
                act.wait_ge(m_xp_ps.sem, m_xp_ps.at(b, 1))
                m_xdbl.by(nc.scalar.copy(xdbl[:, :], ps[0:AUG, 2, :]))

            def m_softplus(b, _):
                for d in range(DT):
                    act.wait_ge(m_dt_ps.sem, m_dt_ps.at(b, d + 1))
                    m_soft.by(nc.scalar.activation(spa[:, d, :], ps[:, 2 + d, :], ACT.Abs, bias=bdt[:, d:d + 1]))
                act.wait_ge(m_soft.sem, m_soft.at(b, 2))
                m_soft.by(nc.scalar.activation(spa[:, :, :], spa[:, :, :], ACT.Exp, scale=-1.0))
                act.wait_ge(m_soft.sem, m_soft.at(b, 3))
                m_soft.by(nc.scalar.activation(spa[:, :, :], spa[:, :, :], ACT.Ln, bias=1.0))

            def scan(b, n):
                if n == 0:
                    act.wait_ge(m_dve.sem, m_dve.at(b, M_DT))
                    if b.first:
                        act.wait_ge(dve_once, DVE_ONCE)
                act.wait_ge(scanned.sem, scanned.at(b, max(DT * (n - 1), 0)))
                for d in range(DT):
                    last = nc.scalar.activation(dA[:, n % 2, d, 1:], dts[:, d, 1:], ACT.Exp, scale=a_neg[:, d, n:n + 1])
                decay.by(last)

            def a_norm(b, _):
                rstd(b, a_rstd, amv, ars, a_dve, A_STAT)

            def qkv(b, _):
                if b.first:
                    act.wait_ge(pool_once, POOL_ONCE)
                act.wait_ge(a_xnt_ps.sem, a_xnt_ps.at(b, 1))
                a_xnt.by(nc.scalar.copy(axnT[:, :], ps[:, 4, :]))
                act.wait_ge(ct_ps.sem, ct_ps.at(b, 1))
                ct_sb.by(nc.scalar.copy(ctxT[:, :], ps[:, 5, 0:P]))
                ct_sb.by(nc.scalar.copy(ctx4[:, :, 0:SK - P], ps[:, 5, P:SK].unsqueeze(1).to_broadcast([P, GH, SK - P])))
                split(b, 0)

            def split(b, a):
                width = (L, SK)[a]
                if a == 0:
                    act.wait_ge(loaded_rest, REST * 16)
                for i, (w, bias) in enumerate(((L, bq[a]), (width, bk[a]))):
                    act.wait_ge(qk_ps.sem, qk_ps.at(b, 2 * a + i + 1))
                    act.wait_ge(qk_parts.sem, qk_parts.at(b, 4 * a))
                    qk_act.by(nc.scalar.activation(qf[:, i, 0:w], ps[:, QK_BANK[i], 0:w], ACT.Identity, bias=bias[:, 0:1]))
                    act.wait_ge(stacked.sem, stacked.at(b, STACKED * a))
                    qk_act.by(nc.scalar.activation(qp[:, i, 0, 0:w], ps[:, QK_BANK[i], 0:w], ACT.Identity, bias=bias[:, 0:1]))
                for i, w in enumerate((L, width)):
                    act.wait_ge(qk_parts.sem, qk_parts.at(b, 4 * a + i + 1))
                    qk_act.by(nc.scalar.copy(qp[:, i, 1, 0:w], qr[:, i, 0:w]))

            def negm_rows(b, a):
                act.wait_ge(nm_ps.sem, nm_ps.at(b, a + 1))
                act.wait_ge(nm_in.sem, nm_in.at(b, 16 * a))
                nm_sb.by(nc.scalar.copy(nmT[:, :], ps[0:PARTS * H, 4, :]))

            def exp(b, r):
                h, (at, w, _) = r // 3, PT_UNITS[r % 3]
                act.wait_ge(pv_ps.sem, pv_ps.at(b, (h - PT_HEADS) // GH + 1 if h >= PT_HEADS else 0))
                act.wait_ge(sc_ps.sem, sc_ps.at(b, r + 1))
                probs.by(nc.scalar.activation(pth[:, h % PT_HEADS, at:at + w], ps[:, 4 + r % 2, 0:w], ACT.Exp, scale=SCALE))

            def cexp(b, m):
                g, r = m // (GH + 1), 3 * H + m
                act.wait_ge(pv_ps.sem, pv_ps.at(b, H // GH + g - 1))
                act.wait_ge(sc_ps.sem, sc_ps.at(b, r + 1))
                probs.by(nc.scalar.activation(cross(g, m % (GH + 1)), ps[:, 4 + r % 2, :], ACT.Exp, scale=SCALE))

            def o_norm(b, a):
                act.wait_ge(oT_ps.sem, oT_ps.at(b, a + 1))
                oT_sb.by(nc.scalar.copy(oT[:, :], ps[:, 4, :]))

            def q2(b, _):
                act.wait_ge(hT_ps.sem, hT_ps.at(b, 1))
                hT_sb.by(nc.scalar.activation(hT[:, :], ps[:, 5, :], ACT.Identity, bias=bocol[0][:, 0:1]))
                split(b, 1)

            def f_norm(b, _):
                rstd(b, f_rstd, fmv, frs, f_dve, F_STAT)

            def f_logits(b, _):
                act.wait_ge(f_xnt_ps.sem, f_xnt_ps.at(b, 1))
                f_xnt.by(nc.scalar.copy(fxnT[:, :], ps[:, 7, :]))

            def f_logits2(b, _):
                act.wait_ge(f_dve.sem, f_dve.at(b, F_LOGITS))
                lg_exp.by(nc.scalar.activation(lex[:, :, :], lg[:, :, :], ACT.Exp))

            def f_route(b, _):
                act.wait_ge(wt_ps.sem, wt_ps.at(b, 1))
                wt_sb.by(nc.scalar.copy(wteT[:, :], ps[0:E, 7, :]))

            def up(b, c):
                if c >= H1_RING:
                    act.wait_ge(ye_ps.sem, ye_ps.at(b, (c - H1_RING) // FC + 1))
                act.wait_ge(h1_ps.sem, h1_ps.at(b, c + 1))
                h1_act.by(nc.scalar.activation(h1[:, c % H1_RING, :], ps[:, c % 2, :], ACT.Relu,
                                               bias=b1c[:, c // FC, c % FC:c % FC + 1]))

            walk(act, {"m_norm": m_norm, "m_in": m_in, "m_conv": m_conv, "m_proj": m_proj, "m_soft": m_softplus, "scan": scan,
                  "a_norm": a_norm, "qkv": qkv, "negm": negm_rows, "exp": exp, "o_norm": o_norm,
                  "q2": q2, "cexp": cexp, "f_norm": f_norm, "f_logits": f_logits, "f_logits2": f_logits2, "f_route": f_route,
                  "up": up})

        @block.vector
        def _(dve):
            nc.vector.memset(eps[:, :], EPS).then_inc(dve_once, 1)
            nc.vector.memset(dA[:, :, :, 0:1], 0.0).then_inc(dve_once, 1)
            nc.vector.memset(w_dt[RANK:AUG, :], 0.0).then_inc(dve_once, 1)
            dve.wait_ge(pool_once, POOL_EARLY)
            nc.vector.tensor_copy(identb[:, :], ident[:, :]).then_inc(dve_once, 1)
            dve.wait_ge(dve_once, DVE_EARLY)

            def norm_stats(b, sig, src, st, mv, between):
                for t in range(T):
                    sig.by(nc.vector.bn_stats(st[:, t, :], src[:, t, :]))
                sig.settle(dve, b)
                sig.by(between())
                for t in range(T):
                    sig.by(nc.vector.bn_aggr(mv[:, t, :], st[:, t, :]))
                sig.settle(dve, b)

            def norm_scale(b, sig, have, src, mv, rs, to):
                dve.wait_ge(have.sem, have.at(b, 2))
                for t in range(T):
                    sig.by(nc.vector.tensor_scalar(to[:, t, :], src[:, t, :], mv[:, t, 0:1], rs[:, t:t + 1],
                                                   ALU.subtract, ALU.mult))

            def m_norm(b, _):
                m_dve.start()
                dve.wait_ge(x_in.sem, x_in.at(b, 16))
                norm_stats(b, m_dve, x_tok, mst, mmv,
                           lambda: nc.vector.memset(xin[:, :, 0:CONV - 1], 0.0))


            def m_norm2(b, _):
                norm_scale(b, m_dve, m_rstd, x_tok, mmv, mrs, mxn)
                if b.first:
                    dve.wait_ge(loaded, FIRST * 16)
                    for j in range(PARTS):
                        nc.vector.tensor_copy(w_bc[:, :, j, :], w_xp[:, :, RANK:AUG]).then_inc(dve_once, 1)
                    dve.wait_ge(act_once, 1)
                    nc.vector.tensor_scalar(a_neg[:, :, :], a_neg[:, :, :], -1.0, None, ALU.mult).then_inc(dve_once, 1)
                    dve.wait_ge(dve_once, DVE_ONCE)

            def m_conv(b, _):
                for d in range(DT):
                    dve.wait_ge(m_xin.sem, m_xin.at(b, d + 1))
                    m_dve.by(nc.vector.tensor_scalar(conv[:, d, :], xin[:, d, 0:L], cw[:, d, 0:1], cb[:, d:d + 1],
                                                     ALU.mult, ALU.add))
                for k in range(1, CONV):
                    for d in range(DT):
                        m_dve.settle(dve, b, 1)
                        m_dve.by(nc.vector.scalar_tensor_tensor(out=conv[:, d, :], in0=xin[:, d, k:k + L],
                                                                scalar=cw[:, d, k:k + 1], in1=conv[:, d, :],
                                                                op0=ALU.mult, op1=ALU.add))
                assert m_dve.here == M_CONV

            def m_proj(b, _):
                dve.wait_ge(m_xp_ps.sem, m_xp_ps.at(b, 2))
                m_dve.by(nc.vector.tensor_copy(bcs[:, :], ps[0:AUG, 3, :]))
                m_dve.settle(dve, b)
                m_dve.by(nc.vector.tensor_tensor(bcr[:, :], ps[0:AUG, 3, :], bcs[:, :], ALU.subtract))
                m_dve.settle(dve, b)
                m_dve.by(nc.vector.tensor_copy(bcs[32:64, :], bcr[32:64, :]))
                m_dve.by(nc.vector.tensor_copy(bcm[64:96, :], bcr[64:96, :]))
                m_dve.settle(dve, b)
                m_dve.by(nc.vector.tensor_tensor(bcs[64:96, :], bcr[64:96, :], bcm[64:96, :], ALU.subtract))
                assert m_dve.here == M_BC

            def m_softplus(b, _):
                for d in range(DT):
                    dve.wait_ge(m_soft.sem, m_soft.at(b, d + 1))
                    m_dve.by(nc.vector.tensor_scalar(dts[:, d, :], ps[:, 2 + d, :], bdt[:, d:d + 1], 0.0, ALU.add, ALU.max))
                dve.wait_ge(m_soft.sem, m_soft.at(b, 4))
                m_dve.settle(dve, b)
                m_dve.by(nc.vector.tensor_tensor(dts[:, :, :], dts[:, :, :], spa[:, :, :], ALU.add))
                assert m_dve.here == M_DT
                m_dve.settle(dve, b)
                dve.wait_ge(m_silu.sem, m_silu.at(b, 2))
                m_dve.by(nc.vector.tensor_tensor(u[:, :, :], dts[:, :, :], xc[:, :, :], ALU.mult))
                m_dve.settle(dve, b)
                drive(b, 0)

            def drive(b, n):
                dve.wait_ge(b_bc.sem, b_bc.at(b, n + 1))
                dve.wait_ge(summed.sem, summed.at(b, max(n - RING + 1, 0)))
                driven.by(nc.vector.tensor_tensor(st[:, n % RING, :, :], u[:, :, :],
                                                  ps[:, 2, :].unsqueeze(1).to_broadcast([P, DT, L]), ALU.mult))

            def scan(b, n):
                dve.wait_ge(decay.sem, decay.at(b, n + 1))
                dve.wait_ge(driven.sem, driven.at(b, n + 1))
                for d in range(DT):
                    scanned.by(nc.vector.tensor_tensor_scan(st[:, n % RING, d, :], dA[:, n % 2, d, :], st[:, n % RING, d, :],
                                                            0.0, ALU.mult, ALU.add))

            def weigh(b, n):
                dve.wait_ge(c_bc.sem, c_bc.at(b, n + 1))
                dve.wait_ge(scanned.sem, scanned.at(b, DT * (n + 1)))
                weighed.by(nc.vector.tensor_tensor(st[:, n % RING, :, :], st[:, n % RING, :, :],
                                                   ps[:, 3, :].unsqueeze(1).to_broadcast([P, DT, L]), ALU.mult))

            def m_out(b, _):
                dve.wait_ge(summed.sem, summed.at(b, N))
                for d in range(DT):
                    m_dve.by(nc.vector.scalar_tensor_tensor(out=yz[:, d, :], in0=xc[:, d, :], scalar=dp[:, d:d + 1],
                                                            in1=ysum[:, d, :], op0=ALU.mult, op1=ALU.add))
                dve.wait_ge(m_silu.sem, m_silu.at(b, 1))
                m_dve.settle(dve, b)
                m_dve.by(nc.vector.tensor_tensor(yz[:, :, :], yz[:, :, :], sz[:, :, :], ALU.mult))
                assert m_dve.here == M_YZ

            def m_out2(b, _):
                dve.wait_ge(m_out_ps.sem, m_out_ps.at(b, 1))
                m_x1.by(nc.vector.tensor_tensor(x_tok[:, :, :], x_tok[:, :, :], ps[:, 2, :].rearrange("p (t d) -> p t d", t=T), ALU.add))

            def a_norm(b, _):
                a_dve.start()
                if b.first:
                    dve.wait_ge(pool_once, POOL_ONCE)
                dve.wait_ge(m_x1.sem, m_x1.at(b, 1))
                if not b.first:
                    dve.wait_ge(f_dve.sem, f_dve.at(b, T + 1 - f_dve.per_batch))
                norm_stats(b, a_dve, x_tok, ast, amv, lambda: nc.vector.tensor_copy(x1[:, :, :], x_tok[:, :, :]))
                assert a_dve.here == A_STAT

            def a_norm2(b, _):
                norm_scale(b, a_dve, a_rstd, x1, amv, ars, axn)
                assert a_dve.here == A_XN

            def qkv(b, _):
                dve.wait_ge(loaded_rest, REST * 16)
                dve.wait_ge(v_ps.sem, v_ps.at(b, 1))
                dve.wait_ge(pv_ps.sem, pv_ps.at(b, 0))
                for t in range(T):
                    a_dve.by(nc.vector.tensor_tensor(v1a[:, t, :, 0:HD], ps[:, 4, t * P:(t + 1) * P].rearrange("p (h e) -> p h e", h=H),
                                                     bvrow[0][:, :].rearrange("p (h e) -> p h e", h=H), ALU.add))
                assert a_dve.here == A_V1

            def smax(b, g):
                i, h0, n = SELF_MAX[g]
                dve.wait_ge(s_max_ps.sem, s_max_ps.at(b, g + 1))
                s_max.by(nc.vector.tensor_reduce(negm[:, i, h0:h0 + n],
                                                 ps[:, 4 + g % 3, :].rearrange("p (c k) -> p c k", k=P * (i + 1))
                                                 if n * P * (i + 1) == L else ps[:, 4 + g % 3, 0:P * (i + 1)].unsqueeze(1),
                                                 AX.X, ALU.max, negate=True))

            def cmax(b, g):
                i, h0, n = CROSS_MAX[g]
                dve.wait_ge(s_max_ps.sem, s_max_ps.at(b, len(SELF_MAX) + g + 1))
                s_max.by(nc.vector.tensor_reduce(negm[:, i, h0:h0 + n],
                                                 ps[:, 4 + g % 3, 0:n * SK].rearrange("p (c k) -> p c k", k=SK),
                                                 AX.X, ALU.max, negate=True))

            def negm_rows(b, a):
                dve.wait_ge(s_max.sem, s_max.at(b, (len(SELF_MAX), len(SELF_MAX) + len(CROSS_MAX))[a]))
                a_dve.by(nc.vector.tensor_copy(nmp[:, :, 0, :], negm[:, :, :]))
                a_dve.settle(dve, b)
                a_dve.by(nc.vector.tensor_tensor(nmr[:, :, :], negm[:, :, :], nmp[:, :, 0, :], ALU.subtract))
                a_dve.settle(dve, b)
                a_dve.by(nc.vector.tensor_copy(nmp[:, :, 1, :], nmr[:, :, :]))
                a_dve.settle(dve, b)
                a_dve.by(nc.vector.tensor_tensor(nmp[:, :, 2, :], nmr[:, :, :], nmp[:, :, 1, :], ALU.subtract))
                a_dve.settle(dve, b)
                assert a_dve.here == A_NM[a]

            def take_pv(b, a, g):
                n = a * (H // GH) + g
                dve.wait_ge(pv_ps.sem, pv_ps.at(b, n + 1))
                dve.wait_ge(ot_ps.sem, ot_ps.at(b, T * a))
                pv_sb.by(nc.vector.tensor_copy(ot[:, g, :], ps[:, 6, :]))

            def exp(b, r):
                if r >= 3 * GH and r % (3 * GH) == 6:
                    take_pv(b, 0, r // (3 * GH) - 1)

            def cexp(b, m):
                if m > GH and m % (GH + 1) == 3:
                    take_pv(b, 1, m // (GH + 1) - 1)

            def o_norm(b, a):
                for i in range(T):
                    dve.wait_ge(ot_ps.sem, ot_ps.at(b, T * a + i + 1))
                    o = ps[:, 4 + i % 3, :].rearrange("p (h x) -> p h x", x=32)
                    a_dve.by(nc.vector.reciprocal(orc[:, i, :].unsqueeze(2), o[:, :, HD:HD + 1]))
                    a_dve.settle(dve, b)
                    o_tok.by(nc.vector.tensor_tensor(otok[:, i, :].rearrange("p (h e) -> p h e", h=H), o[:, :, 0:HD],
                                                     orc[:, i, :].unsqueeze(2).to_broadcast([P, H, HD]), ALU.mult))

            def o_out(b, _):
                dve.wait_ge(o2_ps.sem, o2_ps.at(b, 1))
                a_dve.by(nc.vector.tensor_tensor(x1[:, :, :], x1[:, :, :], ps[:, 5, :].rearrange("p (t d) -> p t d", t=T), ALU.add))
                a_dve.settle(dve, b)
                a_x2.by(nc.vector.tensor_tensor(x1[:, :, :], x1[:, :, :], bo2row[:, :].unsqueeze(1).to_broadcast([P, T, D]), ALU.add))
                assert a_dve.here == A_OUT

            def q2(b, _):
                dve.wait_ge(v_ps.sem, v_ps.at(b, 2))
                a_dve.by(nc.vector.tensor_tensor(v2a[:, :, 0:HD], ps[:, 4, 0:P].rearrange("p (h e) -> p h e", h=H),
                                                 bvrow[1][:, :].rearrange("p (h e) -> p h e", h=H), ALU.add))
                for c in range(GH):
                    rows = slice(32 * c, 32 * c + SK - P)
                    a_dve.by(nc.vector.tensor_tensor(
                        v2b[rows, :, :].rearrange("p (g c) x -> p g c x", c=GH)[:, :, c, 0:HD],
                        ps[rows, 4, P:2 * P].rearrange("p (g c e) -> p g c e", c=GH, e=HD)[:, :, c, :],
                        bvrow[1][rows, :].rearrange("p (g c e) -> p g c e", c=GH, e=HD)[:, :, c, :], ALU.add))
                a_dve.settle(dve, b)
                assert a_dve.here == A_V2

            def f_norm(b, _):
                f_dve.start()
                dve.wait_ge(a_x2.sem, a_x2.at(b, 1))
                dve.wait_ge(acc_free.sem, acc_free.at(b, 16))
                norm_stats(b, f_dve, x1, fst, fmv, lambda: nc.vector.tensor_copy(acc[:, :, :], x1[:, :, :]))
                assert f_dve.here == F_STAT

            def f_norm2(b, _):
                norm_scale(b, f_dve, f_rstd, acc, fmv, frs, fxn)
                assert f_dve.here == F_XN

            def route(b, part):
                chain = lambda ins: (f_dve.by(ins), f_dve.settle(dve, b))
                wide = lambda col: col[:, :].unsqueeze(2).to_broadcast([P, T, E])
                row = lambda r: r[:, :].unsqueeze(1).to_broadcast([P, T, E])
                if part == 0:
                    dve.wait_ge(lg_ps.sem, lg_ps.at(b, 1))
                    chain(nc.vector.tensor_tensor(lg[:, :, :], ps[:, 7, 0:T * E].rearrange("p (t e) -> p t e", t=T), row(brrow), ALU.add))
                    chain(nc.vector.tensor_reduce(lmx[:, :], lg[:, :, :], AX.X, ALU.max))
                    chain(nc.vector.tensor_tensor(lg[:, :, :], lg[:, :, :], wide(lmx), ALU.subtract))
                    assert f_dve.here == F_LOGITS
                elif part == 1:
                    chain(nc.vector.tensor_scalar(oneh[:, :, :], lg[:, :, :], 0.0, None, ALU.is_equal))
                    chain(nc.vector.tensor_tensor(oneh[:, :, :], oneh[:, :, :], row(prefer), ALU.mult))
                    chain(nc.vector.tensor_reduce(lmx[:, :], oneh[:, :, :], AX.X, ALU.max))
                    chain(nc.vector.tensor_tensor(oneh[:, :, :], oneh[:, :, :], wide(lmx), ALU.is_equal))
                    dve.wait_ge(lg_exp.sem, lg_exp.at(b, 1))
                    chain(nc.vector.tensor_reduce(lsm[:, :], lex[:, :, :], AX.X, ALU.add))
                    chain(nc.vector.reciprocal(gate[:, :], lsm[:, :]))
                    chain(nc.vector.tensor_tensor(wte[:, :, :], oneh[:, :, :], wide(gate), ALU.mult))
                    assert f_dve.here == F_WT
                else:
                    dve.wait_ge(b2_ps.sem, b2_ps.at(b, 1))
                    chain(nc.vector.tensor_tensor(acc[:, :, :], acc[:, :, :], ps[:, 7, :].rearrange("p (t d) -> p t d", t=T), ALU.add))
                    assert f_dve.here == F_ACC

            def add_expert(b, n):
                if n % T < T - 1:
                    return
                e = n // T
                dve.wait_ge(ye_ps.sem, ye_ps.at(b, e + 1))
                if e:
                    dve.wait_ge(ye_acc.sem, ye_acc.at(b, e))
                for t in range(T):
                    last = nc.vector.scalar_tensor_tensor(out=acc[:, t, :], in0=ps[:, 7, t * P:(t + 1) * P],
                                                          scalar=wte[:, t, e:e + 1], in1=acc[:, t, :],
                                                          op0=ALU.mult, op1=ALU.add)
                ye_acc.by(last)

            walk(dve, {"m_norm": m_norm, "m_norm2": m_norm2, "m_conv": m_conv, "m_proj": m_proj,
                  "m_soft": m_softplus, "scan": scan,
                  "drive": drive, "weigh": weigh, "m_out": m_out, "m_out2": m_out2,
                  "a_norm": a_norm, "a_norm2": a_norm2, "qkv": qkv, "smax": smax, "negm": negm_rows, "exp": exp,
                  "pv": lambda b, g: take_pv(b, 0, g), "o_norm": o_norm, "q2": q2, "cmax": cmax, "cexp": cexp,
                  "cpv": lambda b, g: take_pv(b, 1, g), "o_out": o_out,
                  "f_norm": f_norm, "f_norm2": f_norm2, "f_logits2": lambda b, _: route(b, 0),
                  "f_route": lambda b, _: route(b, 1), "f_bias": lambda b, _: route(b, 2), "down": add_expert})

        @block.tensor
        def _(pe):
            mm = nc.tensor.matmul
            pe.wait_ge(pool_once, POOL_EARLY)
            pe.wait_ge(dve_once, DVE_EARLY)

            def tr(to, src, n=P):
                return nc.tensor.transpose(to, src, ident[0:n, 0:n])

            def m_norm(b, _):
                pe.wait_ge(m_dve.sem, m_dve.at(b, M_XN))
                pe.wait_ge(m_x1.sem, m_x1.at(b, 0))
                for t in range(T):
                    last = tr(ps[:, 2, t * P:(t + 1) * P], mxn[:, t, :])
                m_xnt_ps.by(last)

            def m_in(b, _):
                if b.first:
                    pe.wait_ge(loaded, FIRST * 16)
                pe.wait_ge(m_xnt.sem, m_xnt.at(b, 1))
                for c in range(2 * DT):
                    if c >= DT:
                        pe.wait_ge(m_xin.sem, m_xin.at(b, c - DT + 1))
                    m_xz.by(mm(ps[:, 2 + c % DT, :], w_in[:, c * P:(c + 1) * P], mxnT[:, :], start=True, stop=True))

            def m_proj(b, _):
                if b.first:
                    pe.wait_ge(dve_once, DVE_ONCE)
                pe.wait_ge(m_silu.sem, m_silu.at(b, 2))
                for d in range(DT):
                    last = mm(ps[0:AUG, 2, :], w_xp[:, d, :], xc[:, d, :], start=(d == 0), stop=(d == DT - 1))
                m_xp_ps.by(last)
                for d in range(DT):
                    last = mm(ps[0:AUG, 3, :], w_bc[:, d, :, :].rearrange("p j n -> p (j n)"), xc[:, d, :],
                              start=(d == 0), stop=(d == DT - 1))
                m_xp_ps.by(last)
                pe.wait_ge(m_xdbl.sem, m_xdbl.at(b, 1))
                for d in range(DT):
                    if d:
                        pe.wait_ge(m_dve.sem, m_dve.at(b, M_CONV + 2))
                    m_dt_ps.by(mm(ps[:, 2 + d, :], w_dt[:, d * P:(d + 1) * P], xdbl[:, :], start=True, stop=True))

            def m_softplus(b, _):
                pe.wait_ge(m_dve.sem, m_dve.at(b, M_BC))
                spread_b(b, 0)

            def spread_b(b, n):
                if n == 0:
                    pe.wait_ge(m_soft.sem, m_soft.at(b, 2))
                    pe.wait_ge(m_dve.sem, m_dve.at(b, M_DT))
                pe.wait_ge(driven.sem, driven.at(b, n))
                b_bc.by(mm(ps[:, 2, :], select[:, n:n + 1].to_broadcast([AUG, P]), bcs[:, :], start=True, stop=True))

            def scan(b, n):
                if n == 0:
                    pe.wait_ge(m_dve.sem, m_dve.at(b, M_DT))
                pe.wait_ge(weighed.sem, weighed.at(b, n))
                c_bc.by(mm(ps[:, 3, :], select[:, N + n:N + n + 1].to_broadcast([AUG, P]), bcs[:, :], start=True, stop=True))

            def m_out(b, _):
                pe.wait_ge(m_dve.sem, m_dve.at(b, M_YZ))
                for t in range(T):
                    for d in range(DT):
                        last = mm(ps[:, 2, t * P:(t + 1) * P], yz[:, d, t * P:(t + 1) * P], w_out[:, d, :],
                                  start=(d == 0), stop=(d == DT - 1))
                m_out_ps.by(last)

            def a_norm2(b, _):
                if b.first:
                    pe.wait_ge(pool_once, POOL_ONCE)
                pe.wait_ge(a_dve.sem, a_dve.at(b, A_XN))
                pe.wait_ge(a_x2.sem, a_x2.at(b, 0))
                for t in range(T):
                    last = tr(ps[:, 4, t * P:(t + 1) * P], axn[:, t, :])
                a_xnt_ps.by(last)
                pe.wait_ge(ctx_in.sem, ctx_in.at(b, 32))
                tr(ps[:, 5, 0:P], ctok[:, 0, :])
                ct_ps.by(tr(ps[:, 5, P:SK], ctok[0:SK - P, 1, :], SK - P))

            def qkv(b, _):
                pe.wait_ge(loaded_rest, REST * 16)
                pe.wait_ge(acc_free.sem, 16)
                pe.wait_ge(a_xnt.sem, a_xnt.at(b, 1))
                qk_ps.by(mm(ps[:, QK_BANK[0], :], wq[0][:, :], axnT[:, :], start=True, stop=True))
                for t in range(T):
                    last = mm(ps[:, 4, t * P:(t + 1) * P], axnT[:, t * P:(t + 1) * P], wv[0][:, :], start=True, stop=True)
                v_ps.by(last)
                pe.wait_ge(ct_sb.sem, ct_sb.at(b, 2))
                qk_ps.by(mm(ps[:, QK_BANK[1], :], wk[0][:, :], axnT[:, :], start=True, stop=True))

            def smax(b, g):
                i, h0, per = SELF_MAX[g]
                w = P * (i + 1)
                if g == 0:
                    pe.wait_ge(stacked.sem, stacked.at(b, STACKED))
                    pe.wait_ge(a_dve.sem, a_dve.at(b, A_V1))
                elif g < 3:
                    pe.wait_ge(qk_act.sem, qk_act.at(b, 4))
                else:
                    pe.wait_ge(s_max.sem, s_max.at(b, g - 2))
                for n in range(per):
                    h, at = h0 + n, n * w
                    mm(ps[:, 4 + g % 3, at:at + w], q_stack[0:AUG, h, i * P:(i + 1) * P], k_stack[0:AUG, h, 0:w],
                       start=(n == 0), stop=False)
                last = mm(ps[:, 4 + g % 3, 0:per * w].rearrange("p (n w) -> p n w", w=w)[:, :, i * P:w], identb[:, :],
                          mask_q[:, :].unsqueeze(1).to_broadcast([P, per, P]), start=False, stop=True)
                s_max_ps.by(last)

            def cmax(b, g):
                i, h0, n = CROSS_MAX[g]
                if g == 0:
                    pe.wait_ge(stacked.sem, stacked.at(b, 2 * STACKED))
                    pe.wait_ge(a_dve.sem, a_dve.at(b, A_V2))
                elif g < 3:
                    pe.wait_ge(qk_act.sem, qk_act.at(b, 10))
                else:
                    pe.wait_ge(s_max.sem, s_max.at(b, len(SELF_MAX) + g - 2))
                for m in range(n):
                    last = mm(ps[:, 4 + g % 3, m * SK:(m + 1) * SK], q_stack[0:AUG, h0 + m, i * P:(i + 1) * P],
                              k2_stack[0:AUG, h0 + m, 0:SK], start=True, stop=True)
                s_max_ps.by(last)

            def negm_rows(b, a):
                pe.wait_ge(a_dve.sem, a_dve.at(b, A_NM[a]))
                for i in range(T):
                    last = mm(ps[0:PARTS * H, 4, i * P:(i + 1) * P], nmp[:, i, :, :].rearrange("p j h -> p (j h)"), identb[:, :],
                              start=True, stop=True)
                nm_ps.by(last)

            def times_v(b, g, tiles=range(T)):
                if tiles[0] == 0:
                    pe.wait_ge(probs.sem, probs.at(b, 3 * GH * (g + 1)))
                    pe.wait_ge(pv_sb.sem, pv_sb.at(b, g))
                for j in tiles:
                    for c in range(GH):
                        last = mm(ps[32 * c:32 * c + 32, 6, j * P:L], v1a[:, j, GH * g + c, :],
                                  pth[:, (GH * g + c) % PT_HEADS, PT_AT[j]:PT_AT[j] + L - j * P], start=(j == 0), stop=(j == T - 1))
                if tiles[-1] == T - 1:
                    pv_ps.by(last)

            def exp(b, r):
                h, (base, _, tiles) = r // 3, PT_UNITS[r % 3]
                if r >= 3 * GH and 3 <= r % (3 * GH) < 3 + T:
                    times_v(b, r // (3 * GH) - 1, [r % (3 * GH) - 3])
                if r == 0:
                    pe.wait_ge(nm_in.sem, nm_in.at(b, 16))
                    pe.wait_ge(nm_sb.sem, nm_sb.at(b, 1))
                elif r >= 2:
                    pe.wait_ge(probs.sem, probs.at(b, r - 1))
                for j in tiles:
                    at, w = PT_AT[j] - base, L - j * P
                    mm(ps[:, 4 + r % 2, at:at + w], k_stack[0:KAUG, h, j * P:(j + 1) * P], q_stack[0:KAUG, h, j * P:L],
                       start=(j == tiles[0]), stop=False)
                firsts = ps[:, 4 + r % 2, :].rearrange("p (n q) -> p n q", q=P)
                firsts = firsts[:, 0:1, :] if len(tiles) == 1 else firsts[:, 0:T:T - 1, :]
                last = mm(firsts, identb[:, :], mask_k[:, :].unsqueeze(1).to_broadcast([P, len(tiles), P]),
                          start=False, stop=True)
                sc_ps.by(last)

            def times_v2(b, g, parts=(0, 1)):
                if parts[0] == 0:
                    pe.wait_ge(probs.sem, probs.at(b, 3 * H + (GH + 1) * (g + 1)))
                    pe.wait_ge(pv_sb.sem, pv_sb.at(b, H // GH + g))
                    for c in range(GH):
                        mm(ps[32 * c:32 * c + 32, 6, :], v2a[:, GH * g + c, :], cross(g, c), start=True, stop=False)
                if parts[-1] == 1:
                    for c in range(GH):
                        last = mm(ps[32 * c:32 * c + 32, 6, :], v2b[:, GH * g + c, :], cross(g, GH), start=False, stop=True)
                    pv_ps.by(last)

            def cexp(b, m):
                g, n = m // (GH + 1), m % (GH + 1)
                r = 3 * H + m
                if g and 1 <= n <= 2:
                    times_v2(b, g - 1, (n - 1,))
                if m == 0:
                    pe.wait_ge(nm_in.sem, nm_in.at(b, 32))
                    pe.wait_ge(nm_sb.sem, nm_sb.at(b, 2))
                elif m >= 2:
                    pe.wait_ge(probs.sem, probs.at(b, r - 1))
                if n < GH:
                    last = mm(ps[:, 4 + r % 2, :], k2_stack[0:KAUG, GH * g + n, 0:P], q_stack[0:KAUG, GH * g + n, :],
                              start=True, stop=True)
                else:
                    for c in range(GH):
                        last = mm(ps[32 * c:32 * c + 32, 4 + r % 2, :], k2_stack[0:KAUG, GH * g + c, P:SKP],
                                  q_stack[0:KAUG, GH * g + c, :], start=True, stop=True)
                sc_ps.by(last)

            def o_norm(b, a):
                pe.wait_ge(pv_sb.sem, pv_sb.at(b, (a + 1) * H // GH))
                pe.wait_ge(probs.sem, probs.at(b, (3 * H, 3 * H + (GH + 1) * H // GH)[a]))
                for i in range(T):
                    if i == 3:
                        pe.wait_ge(o_tok.sem, o_tok.at(b, T * a + 1))
                    for g in range(GH):
                        last = mm(ps[:, 4 + i % 3, g * P:(g + 1) * P], ot[:, g, i * P:(i + 1) * P], ident[:, :], start=True, stop=True)
                    ot_ps.by(last)
                pe.wait_ge(o_tok.sem, o_tok.at(b, T * (a + 1)))
                for i in range(T):
                    last = tr(ps[:, 4, i * P:(i + 1) * P], otok[:, i, :])
                oT_ps.by(last)

            def o_out(b, _):
                pe.wait_ge(oT_sb.sem, oT_sb.at(b, 2))
                for i in range(T):
                    last = mm(ps[:, 5, i * P:(i + 1) * P], oT[:, i * P:(i + 1) * P], wo[1][:, :], start=True, stop=True)
                o2_ps.by(last)

            def q2(b, _):
                pe.wait_ge(oT_sb.sem, oT_sb.at(b, 1))
                hT_ps.by(mm(ps[:, 5, :], wo[0][:, :], oT[:, :], start=True, stop=True))
                pe.wait_ge(ct_sb.sem, ct_sb.at(b, 2))
                mm(ps[:, 4, 0:P], ctxT[:, :], wv[1][:, :], start=True, stop=True)
                v_ps.by(mm(ps[:, 4, P:2 * P], ctx4[:, :, :].rearrange("d c k -> d (c k)"), wv[1][:, :], start=True, stop=True))
                pe.wait_ge(hT_sb.sem, hT_sb.at(b, 1))
                qk_ps.by(mm(ps[:, QK_BANK[0], :], wq[1][:, :], hT[:, :], start=True, stop=True))
                mm(ps[:, QK_BANK[1], 0:P], wk[1][:, :], ctxT[:, :], start=True, stop=True)
                qk_ps.by(mm(ps[:, QK_BANK[1], P:SK], wk[1][:, :], ctx4[:, 0, 0:SK - P], start=True, stop=True))

            def f_norm2(b, _):
                pe.wait_ge(f_dve.sem, f_dve.at(b, F_XN))
                for t in range(T):
                    last = tr(ps[:, 7, t * P:(t + 1) * P], fxn[:, t, :])
                f_xnt_ps.by(last)

            def f_logits(b, _):
                pe.wait_ge(f_xnt.sem, f_xnt.at(b, 1))
                for t in range(T):
                    last = mm(ps[:, 7, t * E:(t + 1) * E], fxnT[:, t * P:(t + 1) * P], wr[:, :], start=True, stop=True)
                lg_ps.by(last)

            def f_route(b, _):
                pe.wait_ge(f_dve.sem, f_dve.at(b, F_WT))
                for t in range(T):
                    last = mm(ps[0:E, 7, t * P:(t + 1) * P], wte[:, t, :], ident[:, :], start=True, stop=True)
                wt_ps.by(last)

            def f_bias(b, _):
                pe.wait_ge(wt_sb.sem, wt_sb.at(b, 1))
                for t in range(T):
                    last = mm(ps[:, 7, t * P:(t + 1) * P], wteT[:, t * P:(t + 1) * P], b2r[:, :], start=True, stop=True)
                b2_ps.by(last)

            def up(b, c):
                e, f = c // FC, c % FC
                if c >= 2:
                    pe.wait_ge(h1_act.sem, h1_act.at(b, c - 1))
                h1_ps.by(mm(ps[:, c % 2, :], w1[:, e, f * P:(f + 1) * P], fxnT[:, :], start=True, stop=True))

            def down(b, n):
                e, t = n // T, n % T
                pe.wait_ge(h1_act.sem, h1_act.at(b, FC * (e + 1)))
                if t == 0 and e:
                    pe.wait_ge(ye_acc.sem, ye_acc.at(b, e))
                elif t == 0:
                    pe.wait_ge(f_dve.sem, f_dve.at(b, F_ACC))
                for f in range(FC):
                    last = mm(ps[:, 7, t * P:(t + 1) * P], h1[:, (FC * e + f) % H1_RING, t * P:(t + 1) * P], w2[:, e, f, :],
                              start=(f == 0), stop=(f == FC - 1))
                if t == T - 1:
                    ye_ps.by(last)

            walk(pe, {"m_norm2": m_norm, "m_in": m_in, "m_proj": m_proj, "m_soft": m_softplus, "scan": scan,
                      "drive": spread_b, "m_out": m_out, "a_norm2": a_norm2, "qkv": qkv, "smax": smax, "negm": negm_rows, "exp": exp, "pv": times_v,
                      "o_norm": o_norm, "q2": q2, "cmax": cmax, "cexp": cexp, "cpv": times_v2, "o_out": o_out,
                      "f_norm2": f_norm2, "f_logits": f_logits, "f_route": f_route, "f_bias": f_bias, "up": up, "down": down})

        for s in signals:
            assert s.seen == 3 * s.per_batch, (s.name, s.seen, s.per_batch)


_INS = ["x", "ctx_1024", "L0_attn_W_in", "L0_attn_conv_w", "L0_attn_conv_b", "L0_attn_W_xproj", "L0_attn_W_dt",
        "L0_attn_b_dt", "L0_attn_A_log", "L0_attn_Dp", "L0_attn_W_out",
        "L0_xattn_Wq1", "L0_xattn_bq1", "L0_xattn_Wk1", "L0_xattn_bk1", "L0_xattn_Wv1", "L0_xattn_bv1",
        "L0_xattn_Wo1", "L0_xattn_bo1", "L0_xattn_Wq2", "L0_xattn_bq2", "L0_xattn_Wk2", "L0_xattn_bk2",
        "L0_xattn_Wv2", "L0_xattn_bv2", "L0_xattn_Wo2", "L0_xattn_bo2",
        "L0_ffn_Wr", "L0_ffn_br", "L0_ffn_W1", "L0_ffn_b1", "L0_ffn_W2", "L0_ffn_b2"]


def kernel(**inputs):
    import numpy as _np
    import concourse.bacc as _bacc
    from concourse import mybir as _mybir
    from concourse.bass_utils import run_bass_kernel_spmd as _run

    nc = _bacc.Bacc("TRN2", target_bir_lowering=False, num_devices=1)
    arrays, args = {}, []
    for name in _INS:
        a = _np.ascontiguousarray(inputs[name])
        arrays[f"in_{name}"] = a
        args.append(nc.dram_tensor(f"in_{name}", a.shape, _mybir.dt.from_np(a.dtype), kind="ExternalInput").ap())
    args.append(nc.dram_tensor("out_x", (B, L, D), _mybir.dt.float32, kind="ExternalOutput").ap())
    decoder_kernel(nc, *args)
    return _run(nc, [arrays], core_ids=[0]).results[0]["out_x"]
```
